# Optimizing a Trainium2 kernel written in Bass

```python
import numpy as np
import jax
import jax.numpy as jnp

def _softmax(x, axis=-1):
    return jax.nn.softmax(x, axis=axis)

def _gelu(x):
    return jax.nn.gelu(x, approximate=True)

def _silu(x):
    return jax.nn.silu(x)

def _sigmoid(x):
    return jax.nn.sigmoid(x)

def _layernorm(x, axis=-1, eps=1e-05):
    m = jnp.mean(x, axis=axis, keepdims=True)
    v = jnp.var(x, axis=axis, keepdims=True)
    return (x - m) / jnp.sqrt(v + eps)

def _scatter_add(tgt, idx, src, axis=0):
    return tgt.at[idx].add(src)

def _segment_sum(src, seg, n):
    return jax.ops.segment_sum(src, seg, n)
kernel_name = 'mk_adaln_d2_jaxref_r4_1e0c80'

def setup_inputs(seed: int=0):
    np.random.seed(seed)
    _w = jnp.asarray

    def _L0_attn_setup():
        import jax, jax.numpy as jnp
        import numpy as np
        import math
        B, S, H = (4, 256, 256)
        NQ, NKV = (16, 8)
        HD = H // NQ
        G = HD * NKV
        DEPTH = 1
        LAMBDA_INIT = 0.8 - 0.6 * math.exp(-0.3 * DEPTH)
        key = jax.random.key(seed)
        ks = jax.random.split(key, 7)
        x = jax.random.normal(ks[0], (B, S, H), jnp.float32)
        Wqkv = jax.random.normal(ks[1], (H, 2 * H + 2 * G), jnp.float32) / math.sqrt(H)
        Wproj = jax.random.normal(ks[2], (H, H), jnp.float32) / math.sqrt(H)
        lambda_q1 = 0.1 * jax.random.normal(ks[3], (G,), jnp.float32)
        lambda_k1 = 0.1 * jax.random.normal(ks[4], (G,), jnp.float32)
        lambda_q2 = 0.1 * jax.random.normal(ks[5], (G,), jnp.float32)
        lambda_k2 = 0.1 * jax.random.normal(ks[6], (G,), jnp.float32)
        return {'x': x, 'Wqkv': Wqkv, 'Wproj': Wproj, 'lambda_q1': lambda_q1, 'lambda_k1': lambda_k1, 'lambda_q2': lambda_q2, 'lambda_k2': lambda_k2}
    _L0_attn_in = _L0_attn_setup()

    def _L0_ffn_setup():
        import jax, jax.numpy as jnp
        import numpy as np
        key = jax.random.key(seed)
        k1, k2, k3, k4, k5 = jax.random.split(key, 5)
        d_in, d_out, r = (256, 256, 32)
        x = jax.random.normal(k1, (8, 2048, d_in), dtype=jnp.float32)
        W = jax.random.normal(k2, (d_out, d_in), dtype=jnp.float32) * (1.0 / np.sqrt(d_in))
        b = jax.random.normal(k3, (d_out,), dtype=jnp.float32) * 0.01
        V_r = jax.random.normal(k4, (d_in, r), dtype=jnp.float32) * (1.0 / np.sqrt(d_in))
        C = jax.random.normal(k5, (d_out, r), dtype=jnp.float32) * (1.0 / np.sqrt(r))
        return {'x': x, 'W': W, 'b': b, 'V_r': V_r, 'C': C}
    _L0_ffn_in = _L0_ffn_setup()
    _L0_c = _w((lambda *s: np.random.randn(*s).astype(np.float32) * 0.05)(2, 256))
    _L0_wmod = _w((lambda *s: np.random.randn(*s).astype(np.float32) * 0.05)(256, 6 * 256) * 256 ** (-0.5))

    def _L1_attn_setup():
        import jax, jax.numpy as jnp
        import numpy as np
        DIM_IN, DIM_OUT, DIM_INNER = (256, 256, 128)
        key = jax.random.key(seed)
        k1, k2, k3, k4 = jax.random.split(key, 4)
        x = jax.random.normal(k1, (4, 512, DIM_IN), dtype=jnp.float32)
        w_qkv = jax.random.uniform(k2, (DIM_INNER * 3, DIM_IN), dtype=jnp.float32, minval=-1.0, maxval=1.0) / np.sqrt(DIM_IN)
        w_out = jax.random.uniform(k3, (DIM_OUT, DIM_INNER), dtype=jnp.float32, minval=-1.0, maxval=1.0) / np.sqrt(DIM_INNER)
        b_out = jax.random.uniform(k4, (DIM_OUT,), dtype=jnp.float32, minval=-1.0, maxval=1.0) / np.sqrt(DIM_INNER)
        return {'x': x, 'w_qkv': w_qkv, 'w_out': w_out, 'b_out': b_out}
    _L1_attn_in = _L1_attn_setup()

    def _L1_ffn_setup():
        import jax, jax.numpy as jnp
        import numpy as np
        S, B, D, H, DH = (1024, 8, 256, 16, 64)

        def _forward(x, Wg, Wq, bq, Wkv, bkv, Wo, bo, ln_g, ln_b):
            s_len, bsz, d_model = x.shape
            n_head, _, d_head = Wq.shape
            cap = s_len // n_head
            scale = 1.0 / d_head ** 0.5
            h = jnp.transpose(x, (1, 0, 2))
            t = h
            probs = jax.nn.softmax(h @ Wg, axis=-1)
            scores = jnp.transpose(probs, (0, 2, 1))
            _, idx = jax.lax.top_k(scores, cap)
            idx = jnp.sort(idx, axis=-1)
            hg = jnp.take_along_axis(h[:, None, :, :], idx[..., None], axis=2)
            hg = jnp.transpose(hg, (1, 0, 2, 3))
            q = jnp.einsum('hbcd,hde->hbce', hg, Wq) + bq[:, None, None, :]
            kv = jnp.einsum('hbcd,hde->hbce', hg, Wkv) + bkv[:, None, None, :]
            k, v = jnp.split(kv, 2, axis=-1)
            att = jnp.einsum('hbid,hbjd->hbij', q, k) * scale
            p = jax.nn.softmax(att, axis=1)
            av = jnp.einsum('hbij,hbjd->hbid', p, v)
            ao = jnp.einsum('hbid,hde->hbie', av, Wo) + bo
            tok = jnp.transpose(idx, (1, 0, 2))
            b_ids = jnp.arange(bsz)[None, :, None]
            outs = jnp.zeros_like(t).at[b_ids, tok].add(ao)
            y = t + outs
            mu = jnp.mean(y, axis=-1, keepdims=True)
            var = jnp.var(y, axis=-1, keepdims=True)
            yn = (y - mu) * jax.lax.rsqrt(var + 1e-05) * ln_g + ln_b
            return jnp.transpose(yn, (1, 0, 2))
        key = jax.random.key(seed)
        ks = jax.random.split(key, 6)
        s = 0.02
        return {'x': jax.random.normal(ks[0], (S, B, D), jnp.float32), 'attn_mask': jnp.zeros((S, S), jnp.bool_), 'Wg': jax.random.normal(ks[1], (D, H), jnp.float32) * s, 'Wq': jax.random.normal(ks[2], (H, D, DH), jnp.float32) * s, 'bq': jnp.zeros((H, DH), jnp.float32), 'Wkv': jax.random.normal(ks[3], (H, D, 2 * DH), jnp.float32) * s, 'bkv': jnp.zeros((H, 2 * DH), jnp.float32), 'Wo': jax.random.normal(ks[4], (H, DH, D), jnp.float32) * s, 'bo': jnp.zeros((D,), jnp.float32), 'ln_g': jnp.ones((D,), jnp.float32), 'ln_b': jnp.zeros((D,), jnp.float32)}
    _L1_ffn_in = _L1_ffn_setup()
    _L1_c = _w((lambda *s: np.random.randn(*s).astype(np.float32) * 0.05)(2, 256))
    _L1_wmod = _w((lambda *s: np.random.randn(*s).astype(np.float32) * 0.05)(256, 6 * 256) * 256 ** (-0.5))
    _d = {'L0_attn_x': _L0_attn_in['x'], 'L0_attn_Wqkv': _L0_attn_in['Wqkv'], 'L0_attn_Wproj': _L0_attn_in['Wproj'], 'L0_attn_lambda_q1': _L0_attn_in['lambda_q1'], 'L0_attn_lambda_k1': _L0_attn_in['lambda_k1'], 'L0_attn_lambda_q2': _L0_attn_in['lambda_q2'], 'L0_attn_lambda_k2': _L0_attn_in['lambda_k2'], 'L0_ffn_W': _L0_ffn_in['W'], 'L0_ffn_b': _L0_ffn_in['b'], 'L0_ffn_V_r': _L0_ffn_in['V_r'], 'L0_ffn_C': _L0_ffn_in['C'], 'L0_c': _L0_c, 'L0_wmod': _L0_wmod, 'L1_attn_w_qkv': _L1_attn_in['w_qkv'], 'L1_attn_w_out': _L1_attn_in['w_out'], 'L1_attn_b_out': _L1_attn_in['b_out'], 'L1_ffn_attn_mask': _L1_ffn_in['attn_mask'], 'L1_ffn_Wg': _L1_ffn_in['Wg'], 'L1_ffn_Wq': _L1_ffn_in['Wq'], 'L1_ffn_bq': _L1_ffn_in['bq'], 'L1_ffn_Wkv': _L1_ffn_in['Wkv'], 'L1_ffn_bkv': _L1_ffn_in['bkv'], 'L1_ffn_Wo': _L1_ffn_in['Wo'], 'L1_ffn_bo': _L1_ffn_in['bo'], 'L1_ffn_ln_g': _L1_ffn_in['ln_g'], 'L1_ffn_ln_b': _L1_ffn_in['ln_b'], 'L1_c': _L1_c, 'L1_wmod': _L1_wmod}
    _x0 = _d['L0_attn_x']
    _d['L0_attn_x'] = jax.random.normal(jax.random.fold_in(jax.random.key(seed), 1), (2, 2048, 256), dtype=_x0.dtype)
    del _x0
    return _d

def reference(L0_attn_x, L0_attn_Wqkv, L0_attn_Wproj, L0_attn_lambda_q1, L0_attn_lambda_k1, L0_attn_lambda_q2, L0_attn_lambda_k2, L0_ffn_W, L0_ffn_b, L0_ffn_V_r, L0_ffn_C, L0_c, L0_wmod, L1_attn_w_qkv, L1_attn_w_out, L1_attn_b_out, L1_ffn_attn_mask, L1_ffn_Wg, L1_ffn_Wq, L1_ffn_bq, L1_ffn_Wkv, L1_ffn_bkv, L1_ffn_Wo, L1_ffn_bo, L1_ffn_ln_g, L1_ffn_ln_b, L1_c, L1_wmod):

    def _L0_attn_ref(x, Wqkv, Wproj, lambda_q1, lambda_k1, lambda_q2, lambda_k2):
        import jax, jax.numpy as jnp
        import numpy as np
        import math
        B, S, H = (4, 256, 256)
        NQ, NKV = (16, 8)
        HD = H // NQ
        G = HD * NKV
        DEPTH = 1
        LAMBDA_INIT = 0.8 - 0.6 * math.exp(-0.3 * DEPTH)
        Bx, Sx, Hx = x.shape
        qkv = x @ Wqkv
        q = qkv[..., :2 * Hx].reshape(Bx, 2 * NQ, Sx, HD)
        k = qkv[..., 2 * Hx:2 * Hx + G].reshape(Bx, NKV, Sx, HD)
        v = qkv[..., 2 * Hx + G:].reshape(Bx, NKV, Sx, HD)
        k = jnp.repeat(k, 2 * NQ // NKV, axis=1)
        v = jnp.repeat(v, NQ // NKV, axis=1)
        scores = jnp.einsum('bhqd,bhkd->bhqk', q, k) / math.sqrt(HD)
        causal = jnp.tril(jnp.ones((Sx, Sx), dtype=bool))
        scores = jnp.where(causal, scores, -jnp.inf)
        aw = jax.nn.softmax(scores, axis=-1)
        lam1 = jnp.exp(jnp.sum(lambda_q1 * lambda_k1))
        lam2 = jnp.exp(jnp.sum(lambda_q2 * lambda_k2))
        lam = lam1 - lam2 + LAMBDA_INIT
        aw = aw.reshape(Bx, NQ, 2, Sx, Sx)
        aw = aw[:, :, 0] - lam * aw[:, :, 1]
        attn = jnp.einsum('bhqk,bhkd->bhqd', aw, v) * (1.0 - LAMBDA_INIT)
        attn = jnp.transpose(attn, (0, 2, 1, 3)).reshape(Bx, Sx, Hx)
        y = attn @ Wproj
        y = jnp.transpose(y, (0, 2, 1)).reshape(Bx, Sx, Hx)
        return y @ Wproj

    def _L0_ffn_ref(x, W, b, V_r, C):
        import jax, jax.numpy as jnp
        import numpy as np
        base = jnp.einsum('bsd,od->bso', x, W) + b
        correction = jnp.einsum('bsr,or->bso', jnp.einsum('bsd,dr->bsr', x, V_r), C)
        return base + correction

    def _L1_attn_ref(x, w_qkv, w_out, b_out):
        import jax, jax.numpy as jnp
        import numpy as np
        DIM_IN, DIM_OUT, DIM_INNER = (256, 256, 128)
        scale = DIM_INNER ** (-0.5)
        qkv = jnp.einsum('bnd,ed->bne', x, w_qkv)
        q, k, v = jnp.split(qkv, 3, axis=-1)
        sim = jnp.einsum('bid,bjd->bij', q, k) * scale
        n = sim.shape[-1]
        causal = jnp.tril(jnp.ones((n, n), dtype=bool))
        sim = jnp.where(causal[None], sim, -jnp.finfo(sim.dtype).max)
        attn = jax.nn.softmax(sim, axis=-1)
        out = jnp.einsum('bij,bjd->bid', attn, v)
        return jnp.einsum('bnd,od->bno', out, w_out) + b_out

    def _L1_ffn_ref(x, attn_mask, Wg, Wq, bq, Wkv, bkv, Wo, bo, ln_g, ln_b):
        import jax, jax.numpy as jnp
        import numpy as np
        S, B, D, H, DH = (1024, 8, 256, 16, 64)

        def _forward(x, Wg, Wq, bq, Wkv, bkv, Wo, bo, ln_g, ln_b):
            s_len, bsz, d_model = x.shape
            n_head, _, d_head = Wq.shape
            cap = s_len // n_head
            scale = 1.0 / d_head ** 0.5
            h = jnp.transpose(x, (1, 0, 2))
            t = h
            probs = jax.nn.softmax(h @ Wg, axis=-1)
            scores = jnp.transpose(probs, (0, 2, 1))
            _, idx = jax.lax.top_k(scores, cap)
            idx = jnp.sort(idx, axis=-1)
            hg = jnp.take_along_axis(h[:, None, :, :], idx[..., None], axis=2)
            hg = jnp.transpose(hg, (1, 0, 2, 3))
            q = jnp.einsum('hbcd,hde->hbce', hg, Wq) + bq[:, None, None, :]
            kv = jnp.einsum('hbcd,hde->hbce', hg, Wkv) + bkv[:, None, None, :]
            k, v = jnp.split(kv, 2, axis=-1)
            att = jnp.einsum('hbid,hbjd->hbij', q, k) * scale
            p = jax.nn.softmax(att, axis=1)
            av = jnp.einsum('hbij,hbjd->hbid', p, v)
            ao = jnp.einsum('hbid,hde->hbie', av, Wo) + bo
            tok = jnp.transpose(idx, (1, 0, 2))
            b_ids = jnp.arange(bsz)[None, :, None]
            outs = jnp.zeros_like(t).at[b_ids, tok].add(ao)
            y = t + outs
            mu = jnp.mean(y, axis=-1, keepdims=True)
            var = jnp.var(y, axis=-1, keepdims=True)
            yn = (y - mu) * jax.lax.rsqrt(var + 1e-05) * ln_g + ln_b
            return jnp.transpose(yn, (1, 0, 2))
        return _forward(x, Wg, Wq, bq, Wkv, bkv, Wo, bo, ln_g, ln_b)
    x = L0_attn_x
    mod = (_silu(L0_c) @ L0_wmod).reshape(L0_c.shape[0], 6, 1, -1)
    sa, ca, ga, sb, cb, gb = (mod[:, 0], mod[:, 1], mod[:, 2], mod[:, 3], mod[:, 4], mod[:, 5])
    ga = (2 * (ga >= 0) - 1) * jnp.maximum(jnp.abs(ga), 0.25)
    gb = (2 * (gb >= 0) - 1) * jnp.maximum(jnp.abs(gb), 0.25)
    h = _layernorm(x, axis=-1) * (1 + ca) + sa
    x = x + ga * _L0_attn_ref(h, L0_attn_Wqkv, L0_attn_Wproj, L0_attn_lambda_q1, L0_attn_lambda_k1, L0_attn_lambda_q2, L0_attn_lambda_k2)
    h = _layernorm(x, axis=-1) * (1 + cb) + sb
    x = x + gb * _L0_ffn_ref(h, L0_ffn_W, L0_ffn_b, L0_ffn_V_r, L0_ffn_C)
    mod = (_silu(L1_c) @ L1_wmod).reshape(L1_c.shape[0], 6, 1, -1)
    sa, ca, ga, sb, cb, gb = (mod[:, 0], mod[:, 1], mod[:, 2], mod[:, 3], mod[:, 4], mod[:, 5])
    ga = (2 * (ga >= 0) - 1) * jnp.maximum(jnp.abs(ga), 0.25)
    gb = (2 * (gb >= 0) - 1) * jnp.maximum(jnp.abs(gb), 0.25)
    h = _layernorm(x, axis=-1) * (1 + ca) + sa
    x = x + ga * _L1_attn_ref(h, L1_attn_w_qkv, L1_attn_w_out, L1_attn_b_out)
    h = _layernorm(x, axis=-1) * (1 + cb) + sb
    x = x + gb * _L1_ffn_ref(h, L1_ffn_attn_mask, L1_ffn_Wg, L1_ffn_Wq, L1_ffn_bq, L1_ffn_Wkv, L1_ffn_bkv, L1_ffn_Wo, L1_ffn_bo, L1_ffn_ln_g, L1_ffn_ln_b)
    return x

_drawn_inputs = setup_inputs


def setup_inputs(seed=0):
    import zlib

    import numpy as np

    out = dict(_drawn_inputs(seed))
    spreads = {'L1_ffn_bq': (0.0, 0.1),
     'L1_ffn_bkv': (0.0, 0.1),
     'L1_ffn_bo': (0.0, 0.1),
     'L1_ffn_ln_g': (1.0, 0.6),
     'L1_ffn_ln_b': (0.0, 2.0)}
    factors = {'L0_attn_Wqkv': 4.028,
     'L0_attn_Wproj': 4.027,
     'L0_attn_lambda_q1': 8.0,
     'L0_attn_lambda_k1': 8.0,
     'L0_attn_lambda_q2': 64.0,
     'L0_attn_lambda_k2': 8.0,
     'L0_ffn_b': 64.0,
     'L1_attn_w_qkv': 64.0,
     'L1_attn_w_out': 64.0,
     'L1_attn_b_out': 40.256,
     'L0_ffn_W': 8.0,
     'L0_ffn_V_r': 8.0,
     'L0_ffn_C': 8.0,
     'L1_c': 8.0,
     'L1_wmod': 8.0}
    for name, (base, spread) in spreads.items():
        noise = np.random.default_rng([zlib.crc32(name.encode()), seed]).standard_normal(out[name].shape)
        drawn = base * np.exp(spread * noise) if base else spread * noise
        out[name] = jnp.asarray(drawn.astype(out[name].dtype))
    for name, factor in factors.items():
        out[name] = (out[name] * factor).astype(out[name].dtype)
    return out
```

```python
import math
from contextlib import ExitStack

import numpy as np

import concourse.bass as bass
from concourse import mybir

ALU = mybir.AluOpType
ACT = mybir.ActivationFunctionType
AX = mybir.AxisListType
F32 = mybir.dt.float32
BF16 = mybir.dt.bfloat16

P = 128
B, S, D = 2, 2048, 256
HD = 16
KV = 8
QH = 4
GROUPS = B * KV
ROWS = S // KV
C = 512
NJ = S // C
TB = C // P
PARTS_Q = (0, 0, 1, 1, 0, 2)
PARTS_K = (0, 1, 0, 1, 2, 0)
KP_ROWS = HD * len(PARTS_Q)
KP_ALL = KP_ROWS + 2
NEG = -3.0e38
EPS = 1e-5
LAMBDA_INIT = 0.8 - 0.6 * math.exp(-0.3)
INNER = 128

B_STEPS = [(j, kt) for j in range(NJ) for kt in range(TB * (j + 1))]
A_STEPS = [(j, t, c) for j in range(NJ) for t in range(TB) for c in range(j + 1)]
STEPS = len(B_STEPS)
LEAD = 19
J_FIRST = [B_STEPS.index((j, 0)) for j in range(NJ)]
J_LAST = [B_STEPS.index((j, TB * (j + 1) - 1)) for j in range(NJ)]
DIAG = [s for s, (j, kt) in enumerate(B_STEPS) if kt >= TB * j]
RING = 3
P_RING = 2

MISC = {5: ["M2"], 7: ["O0"], 8: ["N"], 9: ["W0"], 10: ["W1"], 11: ["W2"], 12: ["W3"], 15: ["O1"],
        19: ["T0"], 20: ["T1"], 21: ["M3", "T2"], 22: ["T3"], 25: ["M0"], 27: ["O2"], 33: ["M1"], 39: ["O3"]}
A_DONE = {4: 2, 20: 3, 24: 0, 32: 1}
PREP = ("N", "W0", "W1", "W2", "W3", "T0", "T1", "T2", "T3")


def uses_of(par, last):
    out = []
    for s in range(STEPS):
        for u in MISC.get(s, []):
            if last and (u in PREP or (par == 1 and u in ("M0", "M1"))):
                continue
            out.append((s, u))
    return out


def width_b(s):
    j, kt = B_STEPS[s]
    return C - P * max(0, kt - TB * j)


def width_a(s):
    j, t, c = A_STEPS[s]
    return P * (t + 1) if c == j else C


class Turns:

    def __init__(self, i, turns=1, n=0):
        self.i, self.turns, self.n = i, turns, n

    def __add__(self, k):
        return Turns(self.i, self.turns, self.n + k)

    def __sub__(self, k):
        return self + -k

    def __mul__(self, k):
        return Turns(self.i, self.turns * k, self.n * k)

    __radd__, __rmul__ = __add__, __mul__


def upto(count):
    return count.i * count.turns + count.n if isinstance(count, Turns) else count


def last_use(unit):
    return min(unit + 1, 2) if unit < 2 else RING


A_INC = 2
LEAD_UNITS = 4 * LEAD
O_AT = {7: 0, 15: 1, 27: 2, 39: 3}
LEAD_DONE = {3: 0, 11: 1}
LEAD_TURN = {5: 0, 13: 1}
PACK_DMAS = (QH + 1) * len(PARTS_Q)
POOL_CONSTS = 13
ROW_MODS = [(0, 0, (2, 5), 0), (0, 1, (2, 5), 0), (1, 0, (2, 3), 2), (1, 0, (4, 5), 4), (1, 1, (2, 3), 2), (1, 1, (4, 5), 4)]


def layer0_attention(nc, sems, keep, x, Wqkv, lq1, lk1, lq2, lk2, c0, wmod0, c1, wmod1):
    ident, mask_a, colmod, rowmod, attn = keep
    with ExitStack() as ctx:
        def sb(name, shape, dt=F32):
            return ctx.enter_context(nc.sbuf_tensor(name, shape, dt))

        def ps(name, shape, dt=F32):
            return ctx.enter_context(nc.psum_tensor(name, shape, dt))

        def sem(name):
            return sems.enter_context(nc.semaphore(name))

        identb = sb("identb", [P, P], BF16)
        cmod = sb("cmod", [P, 2, 2, GROUPS])
        signs = sb("signs", [P, TB, QH])
        spare = sb("spare", [P, 4])
        expo = sb("expo", [P, 8])
        wqkv = sb("wqkv", [P, 2, 3 * D])
        q_pack = [sb(f"q_pack{i}", [P, QH, S], BF16) for i in range(2)]
        k_pack = [sb(f"k_pack{i}", [P, S], BF16) for i in range(2)]
        v_tile = [sb(f"v_tile{i}", [P, S // P, 32]) for i in range(2)]
        probs = sb("probs", [P, P_RING, QH, C])
        xg = sb("xg", [P, 2, D])
        xhat = sb("xhat", [P, 2, D])
        stats = sb("stats", [P, 2, 6])
        mv = sb("mv", [P, 2, 2])
        veps = sb("veps", [P, 2])
        rstd = sb("rstd", [P, 2])
        hT = sb("hT", [P, 2, ROWS])
        qkv_row = sb("qkv_row", [P, 2, 3 * D])
        heads = sb("heads", [P, QH + 1, D])
        heads_by_j = sb("heads_by_j", [P, D // HD, QH + 1, HD])
        headT = sb("headT", [P, S])
        rest = sb("rest", [P, S])
        part = [sb(f"part{i}", [P, S], BF16) for i in range(3)]
        m_part = sb("m_part", [P, QH, TB, NJ])
        m_max = sb("m_max", [P, QH, TB])
        m_neg = sb("m_neg", [P, QH, 2, TB], BF16)
        m_rows = sb("m_rows", [32, P], BF16)
        o_sb = sb("o_sb", [P, C])
        o_rl = sb("o_rl", [P, TB, QH])
        o_w = sb("o_w", [P, TB, QH])
        o_sc = sb("o_sc", [P, 2, TB * QH * HD])
        cT = sb("cT", [P, 2, 2, B])
        cE = sb("cE", [P, 8])
        cS = sb("cS", [P, 2, 2, B])
        cSb = sb("cSb", [P, 2, 2, B, P])
        lam_in = sb("lam_in", [P, 4, P])
        lam = sb("lam", [P, 8])
        wmods = attn[:, :, :, :].rearrange("p g t e -> p (g t e)")[:, 0:6 * D * 4].rearrange(
            "p (l k n) -> p l k n", l=2, k=2)
        gate_t = [probs[:, i, :, :].rearrange("p h q -> p (h q)")[:, 0:4 * D] for i in range(2)]

        products = o_sb[:, 0:2 * P].rearrange("p (l n) -> p l n", l=2)

        a_bank = [ps(f"a_bank{i}", [P, C]) for i in range(RING)]
        b_bank = [ps(f"b_bank{i}", [P, C]) for i in range(RING)]
        acc = ps("acc", [P, C])
        misc = ps("misc", [P, C])
        misc_b = misc[:, :].bitcast(BF16)

        scratch = [nc.dram_tensor(f"scratch{i}", [ROWS * 3 * D], F32, kind="Internal").ap() for i in range(2)]

        pool_consts, dve_consts, act_consts = sem("pool_consts"), sem("dve_consts"), sem("act_consts")
        mod_ready, mod_taken = sem("mod_ready"), sem("mod_taken")
        cT_in, wmod_a_in, wmod_b_in, wqkv_in, lam_inputs = (sem("cT_in"), sem("wmod_a_in"), sem("wmod_b_in"), sem("wqkv_in"),
                                                           sem("lam_inputs"))
        silu_ready, cmod_ready, gate_step, lam_step = sem("silu_ready"), sem("cmod_ready"), sem("gate_step"), sem("lam_step")
        ln_step, m_step, o_step = sem("ln_step"), sem("m_step"), sem("o_step")
        x_loaded, stats_ready, rstd_ready, xhat_ready = sem("x_loaded"), sem("stats_ready"), sem("rstd_ready"), sem("xhat_ready")
        misc_filled = sem("misc_filled")
        hT_ready, rows_ready, rows_out, heads_in, v_in = (sem("hT_ready"), sem("rows_ready"), sem("rows_out"),
                                                          sem("heads_in"), [sem(f"v_in{i}") for i in range(2)])
        heads_ready = sem("heads_ready")
        turned, part0_ready, rest_ready, parts_ready, packs_in = (sem("turned"), sem("part0_ready"), sem("rest_ready"),
                                                                 sem("parts_ready"), sem("packs_in"))
        a_scored, a_maxed, m_ready, m_copied, m_rows_in = (sem("a_scored"), sem("a_maxed"), sem("m_ready"),
                                                          sem("m_copied"), sem("m_rows_in"))
        b_scored, b_exped, b_masked, pv_done = sem("b_scored"), sem("b_exped"), sem("b_masked"), sem("pv_done")
        acc_copied, o_scaled, o_added = sem("acc_copied"), sem("o_scaled"), sem("o_added")
        dve_step = sem("dve_step")

        N_PRO = 20
        PER = 2 * 17

        def a_unit(i, par, s, h):
            return 8 * STEPS * i + 4 * (STEPS * par + s) + h

        def misc_no(i, par, last, s, name):
            n = N_PRO + 1 + (len(uses_of(0, last)) if par else 0) + uses_of(par, last).index((s, name))
            return PER * i + n

        def regions(buf):
            n = ROWS * 2 * D
            return scratch[buf][0:n], scratch[buf][n:n + ROWS * P], scratch[buf][n + ROWS * P:]

        block = ctx.enter_context(nc.Block())

        x_rows = x.rearrange("b s d -> (b s) d")

        @block.sync
        def _(sp):
            for layer, c in enumerate((c0, c1)):
                for n in range(B):
                    sp.dma_start(cT[:, layer, :, n], c[n, :].rearrange("(k p) -> p k", p=P),
                                 allow_slow_non_contiguous=True).then_inc(cT_in, 16)

            def load_x(n, unused):
                if unused is not None:
                    sp.wait_ge(xhat_ready, upto(unused))
                sp.dma_start(xg[:, :, :], x_rows[bass.ds(upto(n * ROWS), ROWS), :].rearrange("(r p) d -> p r d", p=P)) \
                    .then_inc(x_loaded, 16)

            load_x(0, None)
            sp.dma_start(wmods[:, 0, :, 0:2 * D], wmod0.rearrange("(k p) n -> p k n", p=P)[:, :, 0:2 * D]).then_inc(wmod_a_in, 16)
            sp.dma_start(wqkv[:, :, :], Wqkv.rearrange("(k p) n -> p k n", p=P)).then_inc(wqkv_in, 16)
            load_x(1, 1)
            sp.dma_start(wmods[:, 0, :, 2 * D:6 * D], wmod0.rearrange("(k p) n -> p k n", p=P)[:, :, 2 * D:6 * D]).then_inc(wmod_b_in, 16)
            sp.dma_start(wmods[:, 1, :, :], wmod1.rearrange("(k p) n -> p k n", p=P)).then_inc(wmod_b_in, 16)
            for k, v in enumerate((lq1, lk1, lq2, lk2)):
                sp.dma_start(lam_in[:, k, :], v.rearrange("(o n) -> o n", o=1).broadcast_to([P, P])).then_inc(lam_inputs, 16)

            def rows_to_dram(n, buf):
                sp.wait_ge(rows_ready, upto(4 * (n + 1)))
                q, k, v = regions(buf)
                for reg, cols in ((q, slice(0, 2 * D)), (k, slice(2 * D, 2 * D + P)), (v, slice(2 * D + P, 3 * D))):
                    sp.dma_start(reg.rearrange("(r p e) -> p r e", r=2, p=P), qkv_row[:, :, cols]).then_inc(rows_out, 16)

            def heads_from_dram(n, buf, gathered):
                sp.wait_ge(rows_out, upto(48 * (n + 1)))
                if gathered is not None:
                    sp.wait_ge(heads_ready, gathered)
                q, k, _ = regions(buf)
                sp.dma_start(heads[:, 0:QH, :], q.rearrange("(h p e) -> p h e", h=QH, p=P)).then_inc(heads_in, 16)
                sp.dma_start(heads[:, QH, :], k.rearrange("(p e) -> p e", p=P)).then_inc(heads_in, 16)

            def pack(n, buf, steps_done):
                if steps_done is not None:
                    sp.wait_ge(pv_done, upto(steps_done))
                sp.wait_ge(parts_ready, upto(n + 1))
                for r, (pq, pk) in enumerate(zip(PARTS_Q, PARTS_K)):
                    for h in range(QH):
                        sp.dma_start(q_pack[buf][HD * r:HD * (r + 1), h, :], part[pq][HD * h:HD * (h + 1), :]).then_inc(packs_in, 16)
                    sp.dma_start(k_pack[buf][HD * r:HD * (r + 1), :], part[pk][HD * QH:HD * (QH + 1), :]).then_inc(packs_in, 16)
                sp.dma_start(v_tile[buf][:, :, 0:HD], regions(buf)[2].rearrange("(t p d) -> p t d", p=P, d=HD)).then_inc(v_in[buf], 16)

            def maxima_rows(count, buf, j):
                sp.wait_ge(m_copied, upto(count))
                for h in range(QH):
                    sp.dma_start(q_pack[buf][KP_ROWS:KP_ALL, h, C * j:C * (j + 1)], m_rows[2 * TB * h:2 * TB * (h + 1), :]) \
                        .then_inc(m_rows_in, 16)

            rows_to_dram(0, 0)
            heads_from_dram(0, 0, None)
            rows_to_dram(1, 1)
            heads_from_dram(1, 1, 1)
            sp.wait_ge(pool_consts, POOL_CONSTS)
            pack(0, 0, None)
            maxima_rows(1, 0, 0)
            maxima_rows(2, 0, 1)

            def body(i, last):
                for par in range(2):
                    g = 2 * i + par
                    if not last:
                        load_x(g + 2, g + 2)
                    if not (last and par == 1):
                        pack(g + 1, 1 - par, STEPS * g)
                    maxima_rows(4 * g + 3, par, 2)
                    if not last:
                        rows_to_dram(g + 2, par)
                        heads_from_dram(g + 2, par, None)
                    maxima_rows(4 * g + 4, par, 3)
                    if not (last and par == 1):
                        maxima_rows(4 * g + 5, 1 - par, 0)
                        maxima_rows(4 * g + 6, 1 - par, 1)

            with sp.Fori(0, GROUPS // 2 - 1) as i:
                body(Turns(i), False)
            body(GROUPS // 2 - 1, True)

        @block.gpsimd
        def _(pool):
            def made(ins):
                return ins.then_inc(pool_consts, 1)

            made(pool.memset(ident[:, :], 0.0))
            made(pool.memset(identb[:, :], 0.0))
            made(pool.memset(mask_a[:, :], 0.0))
            made(pool.memset(expo[:, :], -0.5))
            pool.wait_ge(pool_consts, 4)
            for m in (ident, identb):
                made(pool.affine_select(out=m[:, :], in_=m[:, :], compare_op=ALU.not_equal, fill=1.0, base=0,
                                        pattern=[[-1, P]], channel_multiplier=1))
            made(pool.affine_select(out=mask_a[:, C - P:C], in_=mask_a[:, C - P:C], compare_op=ALU.is_ge, fill=NEG, base=0,
                                    pattern=[[-1, P]], channel_multiplier=1))
            for buf in range(2):
                made(pool.memset(v_tile[buf][:, :, HD:32], 0.0))
            pool.wait_ge(pool_consts, 9)
            for buf in range(2):
                made(pool.memset(k_pack[buf][KP_ROWS:P, :], 1.0))
            pool.wait_ge(pool_consts, 11)
            for buf in range(2):
                made(pool.memset(v_tile[buf][:, :, HD:HD + 1], 1.0))

            def inverse_deviation(n):
                pool.wait_ge(stats_ready, upto(n + 1))
                if not (isinstance(n, int) and n == 0):
                    pool.wait_ge(xhat_ready, upto(n))
                pool.tensor_tensor(rstd[:, :], veps[:, :], expo[:, 0:2], ALU.pow).then_inc(rstd_ready, 1)

            def split(n):
                pool.wait_ge(part0_ready, upto(n + 1))
                if not (isinstance(n, int) and n == 0):
                    pool.wait_ge(packs_in, upto(16 * PACK_DMAS * n))
                pool.tensor_tensor(rest[0:80, :], headT[0:80, :], part[0][0:80, :], ALU.subtract).then_inc(rest_ready, 1)
                pool.tensor_tensor(part[1][0:80, :], headT[0:80, :], part[0][0:80, :], ALU.subtract).then_inc(rest_ready, 1)
                pool.wait_ge(rest_ready, upto(2 * (n + 1)))
                pool.tensor_tensor(part[2][0:80, :], rest[0:80, :], part[1][0:80, :], ALU.subtract).then_inc(parts_ready, 1)

            inverse_deviation(0)
            inverse_deviation(1)
            split(0)
            split(1)

            def mask(i, par, s):
                j, kt = B_STEPS[s]
                at = P * (kt - TB * j)
                blk = probs[:, s % P_RING, :, at:at + P]
                pool.wait_ge(b_exped, upto(8 * STEPS * i + 4 * (STEPS * par + s) + 4))
                k = DIAG.index(s) % 4
                pool.tensor_tensor(spare[:, k:k + 1], expo[:, 0:1], expo[:, 0:1], ALU.add).then_inc(b_masked, 1)
                pool.affine_select(out=blk, in_=blk, compare_op=ALU.is_ge, fill=0.0, base=0,
                                   pattern=[[0, QH], [1, P]], channel_multiplier=-1).then_inc(b_masked, 1)

            def pair(i, par, j):
                n = 4 * (2 * i + par) + j
                o = o_sc[:, j % 2, :].rearrange("p (t a c e) -> p t a c e", t=TB, a=2, c=2)
                dst = attn[:, bass.ds(upto(2 * i + par), 1), TB * j:TB * (j + 1), :].rearrange("p g t (a e) -> p (g t) a e", a=2)
                pool.wait_ge(o_scaled, upto(n + 1))
                pool.tensor_tensor(dst, o[:, :, :, 0, :], o[:, :, :, 1, :], ALU.add).then_inc(o_added, 1)

            def body(i, last):
                for par in range(2):
                    for s in range(STEPS):
                        if s in DIAG:
                            mask(i, par, s)
                        if s == 3 and not last:
                            inverse_deviation(2 * i + par + 2)
                        if s in O_AT:
                            pair(i, par, O_AT[s])
                        if s == 23 and not last:
                            split(2 * i + par + 2)

            with pool.Fori(0, GROUPS // 2 - 1) as i:
                body(Turns(i), False)
            body(GROUPS // 2 - 1, True)

        @block.vector
        def _(dve):
            dve.wait_ge(act_consts, 1)
            dve.tensor_scalar(cE[:, :], cE[:, :], 1.0, None, ALU.add).then_inc(dve_step, 1)
            dve.wait_ge(dve_step, 1)
            dve.reciprocal(cE[:, :], cE[:, :]).then_inc(dve_step, 1)
            dve.wait_ge(dve_step, 2)
            dve.tensor_tensor(cS[:, :, :, :].rearrange("p l k b -> p (l k b)"), cT[:, :, :, :].rearrange("p l k b -> p (l k b)"),
                              cE[:, :], ALU.mult).then_inc(dve_step, 1)
            dve.wait_ge(dve_step, 3)
            dve.tensor_copy(cSb[:, :, :, :, :].rearrange("p l k b n -> p (l k b) n"),
                            cS[:, :, :, :].rearrange("p l k b -> p (l k b)").unsqueeze(2).broadcast_to([P, 8, P])) \
                .then_inc(silu_ready, 1)

            def normalise(n):
                dve.wait_ge(x_loaded, upto(16 * (n + 1)))
                for r in range(2):
                    dve.bn_stats(stats[:, r, :], xg[:, r, :]).then_inc(ln_step, 1)
                dve.wait_ge(ln_step, upto(5 * n + 2))
                dve.memset(veps[:, :], EPS).then_inc(ln_step, 1)
                for r in range(2):
                    dve.bn_aggr(mv[:, r, :], stats[:, r, :]).then_inc(ln_step, 1)
                dve.wait_ge(ln_step, upto(5 * n + 5))
                dve.tensor_tensor(veps[:, :], mv[:, :, 1], veps[:, :], ALU.add).then_inc(stats_ready, 1)

            def centre(n):
                dve.wait_ge(rstd_ready, upto(n + 1))
                if not (isinstance(n, int) and n == 0):
                    dve.wait_ge(hT_ready, upto(2 * n))
                dve.tensor_scalar(xhat[:, 0, :], xg[:, 0, :], mv[:, 0, 0:1], rstd[:, 0:1], ALU.subtract, ALU.mult)
                dve.tensor_scalar(xhat[:, 1, :], xg[:, 1, :], mv[:, 1, 0:1], rstd[:, 1:2], ALU.subtract, ALU.mult) \
                    .then_inc(xhat_ready, 1)

            def gather_heads(n):
                dve.wait_ge(heads_in, upto(32 * (n + 1)))
                if not (isinstance(n, int) and n == 0):
                    dve.wait_ge(turned, upto(4 * n))
                dve.tensor_copy(heads_by_j[:, :, :, :], heads[:, :, :].rearrange("p h (j d) -> p j h d", d=HD)) \
                    .then_inc(heads_ready, 1)

            normalise(0)
            centre(0)
            dve.wait_ge(mod_ready, 1)
            dve.tensor_copy(colmod[:, 0, :, :], b_bank[0][:, 0:4].rearrange("p (k b) -> p k b", k=2)).then_inc(dve_step, 1)
            dve.tensor_scalar(colmod[:, 1, :, :], b_bank[0][:, 4:8].rearrange("p (k b) -> p k b", k=2), 1.0, None, ALU.add) \
                .then_inc(dve_step, 1)
            dve.wait_ge(dve_step, 5)
            for w in range(2):
                ins = dve.tensor_copy(cmod[:, w, :, :].rearrange("p k (b g) -> p (k b) g", b=B),
                                      colmod[:, w, :, :].rearrange("p k b -> p (k b)").unsqueeze(2).broadcast_to([P, 2 * B, KV]))
                ins.then_inc(cmod_ready, 1)
            normalise(1)
            centre(1)
            dve.wait_ge(mod_ready, 2)
            for w in range(2, 6):
                src = b_bank[1][:, 4 * (w - 2):4 * (w - 1)].rearrange("p (k b) -> p k b", k=2)
                if w % 2:
                    dve.tensor_scalar(colmod[:, w, :, :], src, 1.0, None, ALU.add).then_inc(dve_step, 1)
                else:
                    dve.tensor_copy(colmod[:, w, :, :], src).then_inc(dve_step, 1)
            for n in range(6):
                dve.wait_ge(mod_ready, upto(3 + n))
                _, b, _, at = ROW_MODS[n]
                dve.tensor_copy(rowmod[:, at:at + 2, b, :],
                                (b_bank[2], acc)[n % 2][:, :].rearrange("p (w d) -> p w d", w=2)).then_inc(mod_taken, 1)
            dve.wait_ge(mod_taken, 6)
            for n, w in enumerate((0, 1, 2, 5)):
                g = rowmod[:, w, :, :].rearrange("p b d -> p (b d)")
                t, u = gate_t[0][:, 0:2 * D], gate_t[1][:, 0:2 * D]
                if n:
                    dve.wait_ge(gate_step, 4 * n)
                dve.scalar_tensor_tensor(out=t, in0=g, scalar=-1.0, in1=g, op0=ALU.mult, op1=ALU.max).then_inc(gate_step, 1)
                dve.tensor_scalar(u, g, 0.0, 2.0, ALU.is_ge, ALU.mult).then_inc(gate_step, 1)
                dve.wait_ge(gate_step, 4 * n + 1)
                dve.tensor_scalar(t, t, 0.25, None, ALU.max).then_inc(gate_step, 1)
                dve.wait_ge(gate_step, 4 * n + 3)
                dve.scalar_tensor_tensor(out=g, in0=u, scalar=-1.0, in1=t, op0=ALU.add, op1=ALU.mult).then_inc(gate_step, 1)
            dve.tensor_scalar(rowmod[:, 4, :, :], rowmod[:, 4, :, :], 1.0, None, ALU.add)
            dve.wait_ge(lam_inputs, 64)
            dve.tensor_tensor(products, lam_in[:, 0:4:2, :], lam_in[:, 1:4:2, :], ALU.mult).then_inc(lam_step, 1)
            dve.wait_ge(lam_step, 1)
            dve.tensor_reduce(lam[:, 0:2], products, AX.X, ALU.add).then_inc(lam_step, 1)
            dve.wait_ge(act_consts, 2)
            dve.tensor_tensor(lam[:, 4:5], lam[:, 3:4], lam[:, 2:3], ALU.subtract).then_inc(lam_step, 1)
            dve.wait_ge(lam_step, 3)
            dve.tensor_scalar(lam[:, 5:6], lam[:, 4:5], -LAMBDA_INIT, 1.0 - LAMBDA_INIT, ALU.add, ALU.mult).then_inc(lam_step, 1)
            dve.memset(lam[:, 6:7], 1.0 - LAMBDA_INIT).then_inc(lam_step, 1)
            dve.wait_ge(lam_step, 5)
            dve.tensor_copy(signs[:, :, 0:4:2], lam[:, 6:7].unsqueeze(1).broadcast_to([P, TB, 2])).then_inc(lam_step, 1)
            dve.tensor_copy(signs[:, :, 1:4:2], lam[:, 5:6].unsqueeze(1).broadcast_to([P, TB, 2])).then_inc(lam_step, 1)
            dve.wait_ge(pool_consts, POOL_CONSTS)
            gather_heads(0)
            gather_heads(1)

            def maxima(i, par, s):
                j, t, c = A_STEPS[s % STEPS]
                w = width_a(s % STEPS)
                for h in range(QH):
                    n = a_unit(i, par, s, h)
                    bank = a_bank[a_unit(0, par, s, h) % RING]
                    dve.wait_ge(a_scored, upto(n + 1))
                    if c == j:
                        dve.tensor_tensor_reduce(out=bank[:, 0:w], in0=bank[:, 0:w], in1=mask_a[:, C - w:C], scale=1.0, scalar=NEG,
                                                 op0=ALU.add, op1=ALU.max, accum_out=m_part[:, h, t, c:c + 1]).then_inc(a_maxed, A_INC)
                    else:
                        dve.tensor_reduce(m_part[:, h, t, c:c + 1], bank[:, 0:w], AX.X, ALU.max).then_inc(a_maxed, A_INC)

            def negate(i, par, s, j, m):
                dve.wait_ge(a_maxed, upto(A_INC * a_unit(i, par, s, QH)))
                dve.tensor_reduce(m_max[:, :, :], m_part[:, :, :, 0:j + 1], AX.X, ALU.max).then_inc(m_step, 1)
                dve.wait_ge(m_step, upto(2 * m + 1))
                if not (isinstance(m, int) and m == 0):
                    dve.wait_ge(m_copied, upto(m))
                dve.tensor_scalar(m_neg[:, :, 0, :], m_max[:, :, :], -1.0, None, ALU.mult).then_inc(m_step, 1)
                dve.wait_ge(m_step, upto(2 * m + 2))
                dve.scalar_tensor_tensor(out=m_neg[:, :, 1, :], in0=m_max[:, :, :], scalar=-1.0, in1=m_neg[:, :, 0, :],
                                         op0=ALU.mult, op1=ALU.subtract).then_inc(m_ready, 1)

            def weigh(i, par, last, s, j):
                n = 4 * (2 * i + par) + j
                o = misc[:, :].rearrange("p (t h e) -> p t h e", t=TB, h=QH)
                dve.wait_ge(misc_filled, upto(misc_no(i, par, last, s, f"O{j}")))
                dve.reciprocal(o_rl[:, :, :], o[:, :, :, HD]).then_inc(o_step, 1)
                dve.wait_ge(o_step, upto(2 * n + 1))
                dve.tensor_tensor(o_w[:, :, :], o_rl[:, :, :], signs[:, :, :], ALU.mult).then_inc(o_step, 1)
                dve.wait_ge(o_step, upto(2 * n + 2))
                dve.wait_ge(o_added, upto(n - (1 if par or j else 0)))
                dve.tensor_tensor(o_sc[:, j % 2, :].rearrange("p (t h e) -> p t h e", t=TB, h=QH), o[:, :, :, 0:HD],
                                  o_w[:, :, :].unsqueeze(3).broadcast_to([P, TB, QH, HD]), ALU.mult).then_inc(o_scaled, 1)

            for s in range(LEAD):
                maxima(0, 0, s)
                if s in LEAD_DONE:
                    negate(0, 0, s, LEAD_DONE[s], LEAD_DONE[s])

            def body(i, last):
                for par in range(2):
                    g = 2 * i + par
                    for s in range(STEPS):
                        if not (last and par == 1 and s + LEAD >= STEPS):
                            maxima(i, par, s + LEAD)
                            if s in A_DONE:
                                j = A_DONE[s]
                                negate(i, par, s + LEAD, j, 4 * g + j + (4 if s > 20 else 0))
                        if s in O_AT:
                            weigh(i, par, last, s, O_AT[s])
                        if not last and s == 1:
                            normalise(g + 2)
                        if not last and s == 5:
                            centre(g + 2)
                        if not last and s == 18:
                            gather_heads(g + 2)

            with dve.Fori(0, GROUPS // 2 - 1) as i:
                body(Turns(i), False)
            body(GROUPS // 2 - 1, True)

        @block.scalar
        def _(act):
            act.wait_ge(cT_in, 64)
            act.activation(cE[:, :], cT[:, :, :, :].rearrange("p l k b -> p (l k b)"), ACT.Exp, scale=-1.0).then_inc(act_consts, 1)

            def shift_rows(n, i, par, no):
                act.wait_ge(misc_filled, upto(no))
                if isinstance(n, int) and n == 0:
                    act.wait_ge(cmod_ready, 2)
                for k in range(2):
                    ins = act.activation(hT[:, k, :], misc[:, 2 * P * k:2 * P * (k + 1)], ACT.Identity,
                                         bias=cmod[:, 0, k, bass.ds(upto(n), 1)], scale=cmod[:, 1, k, bass.ds(upto(n), 1)])
                    ins.then_inc(hT_ready, 1)

            def take_rows(n, w, no):
                r, (a, b) = w // 2, ((0, 2 * D), (2 * D, 3 * D))[w % 2]
                if w == 0 and not (isinstance(n, int) and n == 0):
                    act.wait_ge(rows_out, upto(48 * n))
                act.wait_ge(misc_filled, upto(no))
                act.activation(qkv_row[:, r, a:b], misc[:, 0:b - a], ACT.Copy).then_inc(rows_ready, 1)

            def take_heads(n, k, no):
                if k == 0 and not (isinstance(n, int) and n == 0):
                    act.wait_ge(parts_ready, upto(n))
                act.wait_ge(misc_filled, upto(no))
                act.activation(headT[0:80, :].rearrange("q (p j) -> q j p", j=16)[:, 4 * k:4 * (k + 1), :],
                               misc[0:80, :].rearrange("q (j p) -> q j p", j=4), ACT.Copy).then_inc(turned, 1)

            def first_part(n):
                act.wait_ge(turned, upto(4 * (n + 1)))
                if not (isinstance(n, int) and n == 0):
                    act.wait_ge(packs_in, upto(16 * PACK_DMAS * n))
                act.activation(part[0][0:80, :], headT[0:80, :], ACT.Copy).then_inc(part0_ready, 1)

            def take_maxima(m, no):
                act.wait_ge(misc_filled, upto(no))
                if not (isinstance(m, int) and m == 0):
                    act.wait_ge(m_rows_in, upto(64 * m))
                act.activation(m_rows[:, :], misc_b[0:32, 0:P], ACT.Copy).then_inc(m_copied, 1)

            for n in range(2):
                shift_rows(n, 0, 0, 5 * n + 1)
                for w in range(4):
                    take_rows(n, w, 5 * n + 2 + w)
            act.wait_ge(lam_step, 2)
            act.activation(lam[:, 2:4], lam[:, 0:2], ACT.Exp).then_inc(act_consts, 1)
            for n in range(2):
                for k in range(4):
                    take_heads(n, k, 11 + 4 * n + k)
                first_part(n)
            take_maxima(0, 19)
            take_maxima(1, 20)

            def exponentials(i, par, s):
                j, kt = B_STEPS[s]
                w = width_b(s)
                for h in range(QH):
                    unit = 4 * (STEPS * par + s) + h
                    act.wait_ge(b_scored, upto(8 * STEPS * i + unit + 1))
                    if h == 0:
                        act.wait_ge(pv_done, upto(2 * STEPS * i + max(STEPS * par + s - P_RING + 1, 0)))
                    act.activation(probs[:, s % P_RING, h, C - w:C], b_bank[unit % RING][:, 0:w], ACT.Exp, scale=HD ** -0.5) \
                        .then_inc(b_exped, 1)

            def take_output(i, par, j):
                n = 4 * (2 * i + par) + j
                act.wait_ge(pv_done, upto(2 * STEPS * i + STEPS * par + J_LAST[j] + 1))
                act.wait_ge(o_scaled, upto(n))
                act.activation(o_sb[:, :], acc[:, :], ACT.Copy).then_inc(acc_copied, 1)

            def body(i, last):
                for par in range(2):
                    g = 2 * i + par
                    for s in range(STEPS):
                        exponentials(i, par, s)
                        for j in range(NJ):
                            if s == J_LAST[j] + 1 or s == STEPS - 1 == J_LAST[j]:
                                take_output(i, par, j)
                        for use in MISC.get(s, []):
                            if (s, use) not in uses_of(par, last):
                                continue
                            no = misc_no(i, par, last, s, use)
                            if use == "N":
                                shift_rows(g + 2, i, par, no)
                            if use[0] == "W":
                                take_rows(g + 2, int(use[1]), no)
                            if use[0] == "T":
                                take_heads(g + 2, int(use[1]), no)
                            if use[0] == "M":
                                j = int(use[1])
                                take_maxima(4 * g + j + (4 if s > 21 else 0), no)
                            if use == "T3":
                                first_part(g + 2)

            with act.Fori(0, GROUPS // 2 - 1) as i:
                body(Turns(i), False)
            body(GROUPS // 2 - 1, True)

        @block.tensor
        def _(pe):
            def by_feature(bank, layer, cols):
                for w, col in enumerate(cols):
                    for k in range(2):
                        for kc in range(2):
                            at = 4 * w + 2 * k
                            ins = pe.matmul(bank[:, at:at + B], wmods[:, layer[w], kc, D * col + P * k:D * col + P * (k + 1)],
                                            cS[:, layer[w], kc, :], start=kc == 0, stop=kc == 1)
                return ins

            pe.wait_ge(dve_step, 3)
            pe.wait_ge(wmod_a_in, 16)
            by_feature(b_bank[0], (0, 0), (0, 1)).then_inc(mod_ready, 1)

            def turn_rows(n):
                pe.wait_ge(xhat_ready, upto(n + 1))
                for k in range(2):
                    for r in range(2):
                        ins = pe.transpose(misc[:, P * (2 * k + r):P * (2 * k + r + 1)], xhat[:, r, P * k:P * (k + 1)], ident[:, :])
                ins.then_inc(misc_filled, 1)

            def project(n, w):
                r, (a, b) = w // 2, ((0, 2 * D), (2 * D, 3 * D))[w % 2]
                if w == 0 and isinstance(n, int) and n == 0:
                    pe.wait_ge(wqkv_in, 16)
                for k in range(2):
                    ins = pe.matmul(misc[:, 0:b - a], hT[:, k, P * r:P * (r + 1)], wqkv[:, k, a:b], start=k == 0, stop=k == 1)
                ins.then_inc(misc_filled, 1)

            def turn_heads(n, k):
                if k == 0:
                    pe.wait_ge(heads_ready, upto(n + 1))
                for jj in range(4):
                    j = 4 * k + jj
                    ins = pe.transpose(misc[0:80, P * jj:P * (jj + 1)], heads_by_j[:, j, :, :].rearrange("p h d -> p (h d)"), ident[:, :])
                ins.then_inc(misc_filled, 1)

            def turn_maxima(m):
                pe.wait_ge(m_ready, upto(m + 1))
                pe.transpose(misc_b[0:32, 0:P], m_neg[:, :, :, :].rearrange("p h j t -> p (h j t)"), identb[:, :]).then_inc(misc_filled, 1)

            def turn_output(n):
                pe.wait_ge(acc_copied, upto(n + 1))
                for t in range(TB):
                    ins = pe.transpose(misc[:, P * t:P * (t + 1)], o_sb[:, P * t:P * (t + 1)], ident[:, :])
                ins.then_inc(misc_filled, 1)

            def emptied(use, n):
                done, count = {"N": (hT_ready, 2 * n + 2), "W": (rows_ready, n + 1), "T": (turned, n + 1),
                               "M": (m_copied, n + 1), "O": (o_scaled, n + 1)}[use[0]]
                pe.wait_ge(done, upto(count))

            def number(use, s, g):
                k = int(use[1]) if len(use) > 1 else 0
                return {"N": g + 2, "W": 4 * (g + 2) + k, "T": 4 * (g + 2) + k,
                        "M": 4 * g + k + (4 if s > 21 else 0), "O": 4 * g + k}[use[0]]

            def before(i, par, last, s, use):
                uses = uses_of(par, last)
                at = uses.index((s, use))
                g = 2 * i + par
                if at:
                    return uses[at - 1][1], number(uses[at - 1][1], uses[at - 1][0], g)
                return "O3", 4 * g - 1

            for n in range(2):
                if n:
                    emptied("W", 4 * n - 1)
                turn_rows(n)
                for w in range(4):
                    emptied("W" if w else "N", 4 * n + w - 1 if w else n)
                    project(n, w)
            pe.wait_ge(wmod_b_in, 32)
            by_feature(b_bank[1], (0, 0, 1, 1), (3, 4, 0, 1)).then_inc(mod_ready, 1)
            pe.wait_ge(silu_ready, 1)
            for n, (layer, b, cols, _) in enumerate(ROW_MODS):
                if n >= 2:
                    pe.wait_ge(mod_taken, upto(n - 1))
                for w, col in enumerate(cols):
                    for kc in range(2):
                        ins = pe.matmul((b_bank[2], acc)[n % 2][:, D * w:D * (w + 1)], cSb[:, layer, kc, b, :],
                                        wmods[:, layer, kc, D * col:D * (col + 1)], start=kc == 0, stop=kc == 1)
                ins.then_inc(mod_ready, 1)
            for n in range(2):
                for k in range(4):
                    emptied("T" if n or k else "W", 4 * n + k - 1 if n or k else 7)
                    turn_heads(n, k)

            def score_maxima(i, par, s, h):
                j, t, c = A_STEPS[s % STEPS]
                buf = (par + s // STEPS) % 2
                unit = a_unit(0, par, s, h)
                w, q = width_a(s % STEPS), C * j + P * t
                if unit >= LEAD_UNITS:
                    pe.wait_ge(a_maxed, upto(A_INC * (a_unit(i, par, s, h) - last_use(unit - LEAD_UNITS) + 1)))
                elif unit >= RING:
                    pe.wait_ge(a_maxed, upto(A_INC * (unit - RING + 1)))
                pe.matmul(a_bank[unit % RING][:, 0:w], q_pack[buf][0:KP_ROWS, h, q:q + P],
                          k_pack[buf][0:KP_ROWS, C * c:C * c + w], start=True, stop=True).then_inc(a_scored, 1)

            def score(i, par, s, h):
                j, kt = B_STEPS[s]
                unit = 4 * (STEPS * par + s) + h
                w = width_b(s)
                pe.wait_ge(b_exped, upto(8 * STEPS * i + unit - last_use(unit) + 1))
                pe.matmul(b_bank[unit % RING][:, 0:w], k_pack[par][0:KP_ALL, P * kt:P * (kt + 1)],
                          q_pack[par][0:KP_ALL, h, C * (j + 1) - w:C * (j + 1)], start=True, stop=True).then_inc(b_scored, 1)

            def meet_v(i, par, s):
                j, kt = B_STEPS[s]
                g, w = 2 * i + par, width_b(s)
                if s == 0:
                    pe.wait_ge(v_in[par], upto(16 * (i + 1)))
                if kt == 0:
                    pe.wait_ge(acc_copied, upto(4 * g + j))
                pe.wait_ge(b_exped, upto(8 * STEPS * i + 4 * (STEPS * par + s) + 4))
                if s in DIAG:
                    pe.wait_ge(b_masked, upto(2 * (len(DIAG) * g + DIAG.index(s) + 1)))
                for h in range(QH):
                    ins = pe.matmul(acc[32 * h:32 * (h + 1), C - w:C], v_tile[par][:, kt, :], probs[:, s % P_RING, h, C - w:C],
                                    start=kt == 0, stop=kt == TB * (j + 1) - 1, skip_group_check=True)
                ins.then_inc(pv_done, 1)

            pe.wait_ge(packs_in, upto(16 * PACK_DMAS))
            for s in range(LEAD):
                for h in range(QH):
                    score_maxima(0, 0, s, h)
                if s in LEAD_TURN:
                    m = LEAD_TURN[s]
                    emptied("M" if m else "T", m - 1 if m else 7)
                    turn_maxima(m)

            def body(i, last):
                for par in range(2):
                    g = 2 * i + par
                    for s in range(STEPS):
                        j = B_STEPS[s][0]
                        if s == J_FIRST[j]:
                            pe.wait_ge(m_rows_in, upto(16 * QH * (4 * g + j + 1)))
                        ahead = not (last and par == 1 and s + LEAD >= STEPS)
                        if ahead and s + LEAD == STEPS:
                            pe.wait_ge(packs_in, upto(16 * PACK_DMAS * (g + 2)))
                        for h in range(QH):
                            if ahead:
                                score_maxima(i, par, s + LEAD, h)
                            score(i, par, s, h)
                        if s:
                            meet_v(i, par, s - 1)
                        if s == STEPS - 1:
                            meet_v(i, par, s)
                        for use in [u for t, u in uses_of(par, last) if t == s]:
                            emptied(*before(i, par, last, s, use))
                            n = number(use, s, g)
                            if use == "N":
                                turn_rows(n)
                            if use[0] == "W":
                                project(g + 2, int(use[1]))
                            if use[0] == "T":
                                turn_heads(g + 2, int(use[1]))
                            if use[0] == "M":
                                turn_maxima(n)
                            if use[0] == "O":
                                turn_output(n)

            with pe.Fori(0, GROUPS // 2 - 1) as i:
                body(Turns(i), False)
            body(GROUPS // 2 - 1, True)


def layer0_out(nc, sems, keep, x, Wproj, fW, fb, fV, fC, w_qkv, w_out, b_out, ln_g, ln_b):
    ident, colmod, rowmod, attn, x2, h1T, w1T, woT, last_rows = keep
    with ExitStack() as ctx:
        def sb(name, shape, dt=F32):
            return ctx.enter_context(nc.sbuf_tensor(name, shape, dt))

        def sem(name):
            return sems.enter_context(nc.semaphore(name))

        wp = sb("wp", [P, 2, D])
        wp_g = sb("wp_g", [P, B, 2, D])
        f_in = sb("f_in", [P, 2, D])
        fv_in = sb("fv_in", [P, 2, 32])
        fc_in = sb("fc_in", [P, 2, 32])
        fvT = sb("fvT", [32, 2, P])
        fcT = sb("fcT", [32, 2, P])
        w_eff = sb("w_eff", [P, B, 2, D])
        wq_in = sb("wq_in", [P, 3, D])
        wo_in = sb("wo_in", [P, 2, P])
        rows_in = sb("rows_in", [P, 4, D])
        f_bias = sb("f_bias", [P, B, D])
        o_in = sb("o_in", [P, B, 2, D])
        aT = sb("aT", [P, B, 2, 2, P])
        y = sb("y", [P, B, 2, D])
        x1 = sb("x1", [P, B, 2, D])
        x1b = sb("x1b", [P, B, 2, D])
        xh = sb("xh", [P, 2, B, 2, D])
        fT = sb("fT", [P, B, 2, 2, P])
        st = sb("st", [P, 2, B, 2, 6])
        mv = sb("mv2", [P, 2, B, 2, 2])
        ve = sb("ve", [P, 2, B, 2])
        rs = sb("rs", [P, 2, B, 2])
        half = sb("half", [P, 2])
        bank = [[ctx.enter_context(nc.psum_tensor(f"bank{b}{n}", [P, C], F32)) for n in range(4)] for b in range(B)]

        w_loaded, setup_filled, setup_taken, gated, half_set, x_in = (
            sem("w_loaded"), sem("setup_filled"), sem("setup_taken"), sem("gated"), sem("half_set"), sem("x_in"))
        o_copied, a_turned, a_taken, y_made, y_taken, z_made, x1_made, x1b_made = (
            sem("o_copied"), sem("a_turned"), sem("a_taken"), sem("y_made"), sem("y_taken"), sem("z_made"), sem("x1_made"),
            sem("x1b_made"))
        f_turned, f_taken, f_made, x2_made, h_turned, h_taken = (sem("f_turned"), sem("f_taken"), sem("f_made"), sem("x2_made"),
                                                                sem("h_turned"), sem("h_taken"))
        ln_step = [[sem(f"ln_step{n}{b}") for b in range(B)] for n in range(2)]
        ve_made = [[sem(f"ve_made{n}{b}") for b in range(B)] for n in range(2)]
        rs_made = [[sem(f"rs_made{n}{b}") for b in range(B)] for n in range(2)]
        xh_made = [[sem(f"xh_made{n}{b}") for b in range(B)] for n in range(2)]
        NB = S // ROWS
        GATED = 14

        def run(eng, turn):
            turn(0, True, False, False)
            turn(1, True, True, False)
            turn(2, True, True, True)
            with eng.Fori(3, NB) as n:
                turn(Turns(n), True, True, True)
            turn(NB, False, True, True)
            turn(NB + 1, False, False, True)

        def wait_over(eng, s, count):
            if not (isinstance(count, int) and count <= 0):
                eng.wait_ge(s, upto(count))

        block = ctx.enter_context(nc.Block())

        @block.sync
        def _(sp):
            sp.dma_start(wp[:, :, :], Wproj.rearrange("(k p) n -> p k n", p=P)).then_inc(w_loaded, 16)
            sp.dma_start(f_in[:, :, :], fW.rearrange("(k p) n -> p k n", p=P)).then_inc(w_loaded, 16)
            sp.dma_start(fv_in[:, :, :], fV.rearrange("(k p) n -> p k n", p=P)).then_inc(w_loaded, 16)
            sp.dma_start(fc_in[:, :, :], fC.rearrange("(k p) n -> p k n", p=P)).then_inc(w_loaded, 16)
            sp.dma_start(wq_in[:, :, :], w_qkv.rearrange("(k p) n -> p k n", p=P)).then_inc(w_loaded, 16)
            sp.dma_start(wo_in[:, :, :], w_out.rearrange("(k p) n -> p k n", p=P)).then_inc(w_loaded, 16)
            for k, v in enumerate((fb, b_out, ln_g, ln_b)):
                sp.dma_start(rows_in[:, k, :], v.rearrange("(o n) -> o n", o=1).broadcast_to([P, D])).then_inc(w_loaded, 16)
            for b in range(B):
                for k in range(2):
                    sp.dma_start(x2[:, :, b, k, :], x[b, P * NB * k:P * NB * (k + 1), :].rearrange("(c n) d -> c n d", n=NB)) \
                        .then_inc(x_in, 16)

        @block.gpsimd
        def _(pool):
            pool.memset(half[:, :], -0.5).then_inc(half_set, 1)
            pool.wait_ge(half_set, 1)

            def deviation(n, which, b):
                pool.wait_ge(ve_made[which][b], upto(n + 1))
                pool.tensor_tensor(rs[:, which, b, :], ve[:, which, b, :], half[:, :], ALU.pow).then_inc(rs_made[which][b], 1)

            def turn(n, a, bb, c):
                if a:
                    for b in range(B):
                        wait_over(pool, a_turned, 2 * n + b - 1)
                        pool.tensor_copy(o_in[:, b, :, :].rearrange("p t (g e) -> p g t e", g=KV),
                                         attn[:, KV * b:KV * (b + 1), bass.ds(upto(2 * n), 2), :]).then_inc(o_copied, 1)
                    for b in range(B):
                        deviation(n, 0, b)
                if bb:
                    for b in range(B):
                        deviation(n - 1, 1, b)
                if a:
                    pool.wait_ge(gated, GATED)
                    for b in range(B):
                        pool.wait_ge(x1_made, upto(2 * n + b + 1))
                        wait_over(pool, x2_made, 2 * n + b - 1)
                        pool.tensor_tensor(x1b[:, b, :, :], x1[:, b, :, :], f_bias[:, b, :].unsqueeze(1).broadcast_to([P, 2, D]),
                                           ALU.add).then_inc(x1b_made, 1)

            run(pool, turn)

        @block.vector
        def _(dve):
            def gate(out, in0, in1, op=ALU.mult):
                dve.tensor_tensor(out, in0, in1, op).then_inc(gated, 1)

            dve.wait_ge(w_loaded, 160)
            for b in range(B):
                gate(wp_g[:, b, :, :], wp[:, :, :], rowmod[:, 0, b, :].unsqueeze(1).broadcast_to([P, 2, D]))
                gate(f_bias[:, b, :], rows_in[:, 0, :], rowmod[:, 1, b, :])
                gate(last_rows[:, 0, b, :], rows_in[:, 1, :], rowmod[:, 2, b, :])
                gate(last_rows[:, 1, b, :], rows_in[:, 2, :], rowmod[:, 5, b, :])
                gate(last_rows[:, 2, b, :], rows_in[:, 3, :], rowmod[:, 5, b, :])
            dve.wait_ge(setup_filled, 1)
            dve.tensor_copy(fvT[:, :, :], bank[0][0][0:32, 0:2 * P].rearrange("p (k n) -> p k n", k=2)).then_inc(setup_taken, 1)
            dve.tensor_copy(fcT[:, :, :], bank[0][0][0:32, 2 * P:4 * P].rearrange("p (k n) -> p k n", k=2)).then_inc(setup_taken, 1)
            for k in range(2):
                dve.wait_ge(setup_filled, 2 + k)
                dve.tensor_copy(w1T[:, k, :], bank[0][1 + k][:, 0:3 * P]).then_inc(setup_taken, 1)
            dve.wait_ge(setup_filled, 4)
            for b in range(B):
                dve.tensor_tensor(woT[:, b, :], bank[0][3][:, 0:D], rowmod[:, 2, b, :], ALU.mult).then_inc(setup_taken, 1)
            for k in range(2):
                dve.wait_ge(setup_filled, 5 + k)
                for b in range(B):
                    gate(w_eff[:, b, k, :], bank[1][k][:, 0:D], rowmod[:, 1, b, :])
            dve.wait_ge(x_in, 64)

            def moments(n, which, b, src, made):
                s = ln_step[which][b]
                dve.wait_ge(made, upto(2 * n + b + 1))
                dve.memset(ve[:, which, b, 0:1], EPS).then_inc(s, 1)
                for k in range(2):
                    dve.bn_stats(st[:, which, b, k, :], src(k)).then_inc(s, 1)
                dve.wait_ge(s, upto(6 * n + 3))
                dve.memset(ve[:, which, b, 1:2], EPS).then_inc(s, 1)
                for k in range(2):
                    dve.bn_aggr(mv[:, which, b, k, :], st[:, which, b, k, :]).then_inc(s, 1)
                dve.wait_ge(s, upto(6 * n + 6))
                dve.tensor_tensor(ve[:, which, b, :], mv[:, which, b, :, 1], ve[:, which, b, :], ALU.add) \
                    .then_inc(ve_made[which][b], 1)

            def centre(n, which, b, src, used):
                dve.wait_ge(rs_made[which][b], upto(n + 1))
                wait_over(dve, used, 2 * n + b - 1)
                for k in range(2):
                    ins = dve.tensor_scalar(xh[:, which, b, k, :], src(k), mv[:, which, b, k, 0:1], rs[:, which, b, k:k + 1],
                                            ALU.subtract, ALU.mult)
                ins.then_inc(xh_made[which][b], 1)

            def turn(n, a, bb, c):
                slot = lambda m, b: x2[:, bass.ds(upto(m), 1), b, :, :].rearrange("p m k d -> p (m k) d")
                if a:
                    for b in range(B):
                        dve.wait_ge(z_made, upto(2 * n + b + 1))
                        wait_over(dve, x1b_made, 2 * n + b - 1)
                        dve.tensor_tensor(x1[:, b, :, :], bank[b][0][:, :].rearrange("p (k d) -> p k d", k=2), slot(n, b), ALU.add) \
                            .then_inc(x1_made, 1)
                        moments(n, 0, b, lambda k: x1[:, b, k, :], x1_made)
                    for b in range(B):
                        centre(n, 0, b, lambda k: x1[:, b, k, :], f_turned)
                if bb:
                    m = n - 1
                    for b in range(B):
                        dve.wait_ge(f_made, upto(2 * m + b + 1))
                        dve.wait_ge(x1b_made, upto(2 * m + b + 1))
                        dve.tensor_tensor(slot(m, b), bank[b][1][:, :].rearrange("p (k d) -> p k d", k=2), x1b[:, b, :, :], ALU.add) \
                            .then_inc(x2_made, 1)
                        moments(m, 1, b, lambda k: x2[:, bass.ds(upto(m), 1), b, k, :].rearrange("p m d -> p (m d)"), x2_made)
                    for b in range(B):
                        centre(m, 1, b, lambda k: x2[:, bass.ds(upto(m), 1), b, k, :].rearrange("p m d -> p (m d)"), h_turned)

            run(dve, turn)

        @block.scalar
        def _(act):
            def turn(n, a, bb, c):
                if a:
                    for b in range(B):
                        act.wait_ge(a_turned, upto(2 * n + b + 1))
                        act.activation(aT[:, b, :, :, :].rearrange("p k t q -> p (k t q)"), bank[b][0][:, :], ACT.Copy) \
                            .then_inc(a_taken, 1)
                    for b in range(B):
                        act.wait_ge(y_made, upto(2 * n + b + 1))
                        act.activation(y[:, b, :, :].rearrange("p t d -> p (t d)"), bank[b][1][:, :], ACT.Copy).then_inc(y_taken, 1)
                if c:
                    m = n - 2
                    for b in range(B):
                        act.wait_ge(h_turned, upto(2 * m + b + 1))
                        for k in range(2):
                            ins = act.activation(h1T[:, b, k, :].rearrange("p (c n) -> p n c", n=NB)[:, bass.ds(upto(m), 1), :],
                                                 bank[b][2][:, D * k:D * (k + 1)].unsqueeze(1), ACT.Identity,
                                                 bias=colmod[:, 4, k, b:b + 1], scale=colmod[:, 5, k, b:b + 1])
                        ins.then_inc(h_taken, 1)
                if bb:
                    m = n - 1
                    for b in range(B):
                        act.wait_ge(f_turned, upto(2 * m + b + 1))
                        for k in range(2):
                            ins = act.activation(fT[:, b, k, :, :].rearrange("p c q -> p (c q)"), bank[b][3][:, D * k:D * (k + 1)],
                                                 ACT.Identity, bias=colmod[:, 2, k, b:b + 1], scale=colmod[:, 3, k, b:b + 1])
                        ins.then_inc(f_taken, 1)

            run(act, turn)

        @block.tensor
        def _(pe):
            pe.wait_ge(w_loaded, 160)
            for k in range(2):
                pe.transpose(bank[0][0][0:32, P * k:P * (k + 1)], fv_in[:, k, :], ident[:, :])
            for k in range(2):
                ins = pe.transpose(bank[0][0][0:32, P * (2 + k):P * (3 + k)], fc_in[:, k, :], ident[:, :])
            ins.then_inc(setup_filled, 1)
            for k in range(2):
                for e in range(3):
                    ins = pe.transpose(bank[0][1 + k][:, P * e:P * (e + 1)], wq_in[:, e, P * k:P * (k + 1)], ident[:, :])
                ins.then_inc(setup_filled, 1)
            for o in range(2):
                ins = pe.transpose(bank[0][3][:, P * o:P * (o + 1)], wo_in[:, o, :], ident[:, :])
            ins.then_inc(setup_filled, 1)
            pe.wait_ge(setup_taken, 2)
            for k in range(2):
                for o in range(2):
                    cols = bank[1][k][:, P * o:P * (o + 1)]
                    pe.matmul(cols, f_in[:, o, P * k:P * (k + 1)], ident[:, :], start=True, stop=False)
                    ins = pe.matmul(cols, fvT[:, k, :], fcT[:, o, :], start=False, stop=True)
                ins.then_inc(setup_filled, 1)
            pe.wait_ge(gated, GATED)
            pe.wait_ge(setup_taken, 6)

            def turn(n, a, bb, c):
                if a:
                    for b in range(B):
                        pe.wait_ge(o_copied, upto(2 * n + b + 1))
                        wait_over(pe, x1_made, 2 * n + b - 1)
                        for k in range(2):
                            for t in range(2):
                                ins = pe.transpose(bank[b][0][:, P * (2 * k + t):P * (2 * k + t + 1)],
                                                   o_in[:, b, t, P * k:P * (k + 1)], ident[:, :])
                        ins.then_inc(a_turned, 1)
                    for b in range(B):
                        pe.wait_ge(a_taken, upto(2 * n + b + 1))
                        wait_over(pe, x2_made, 2 * n + b - 3)
                        for t in range(2):
                            for k in range(2):
                                ins = pe.matmul(bank[b][1][:, D * t:D * (t + 1)], aT[:, b, k, t, :], wp[:, k, :],
                                                start=k == 0, stop=k == 1)
                        ins.then_inc(y_made, 1)
                if c:
                    m = n - 2
                    for b in range(B):
                        pe.wait_ge(xh_made[1][b], upto(m + 1))
                        wait_over(pe, h_taken, 2 * m + b - 1)
                        for k in range(2):
                            for cc in range(2):
                                ins = pe.transpose(bank[b][2][:, P * (2 * k + cc):P * (2 * k + cc + 1)],
                                                   xh[:, 1, b, cc, P * k:P * (k + 1)], ident[:, :])
                        ins.then_inc(h_turned, 1)
                if bb:
                    m = n - 1
                    for b in range(B):
                        pe.wait_ge(xh_made[0][b], upto(m + 1))
                        wait_over(pe, f_taken, 2 * m + b - 1)
                        for k in range(2):
                            for cc in range(2):
                                ins = pe.transpose(bank[b][3][:, P * (2 * k + cc):P * (2 * k + cc + 1)],
                                                   xh[:, 0, b, cc, P * k:P * (k + 1)], ident[:, :])
                        ins.then_inc(f_turned, 1)
                if a:
                    for b in range(B):
                        pe.wait_ge(y_taken, upto(2 * n + b + 1))
                        for cc in range(2):
                            for t in range(2):
                                ins = pe.matmul(bank[b][0][:, D * cc:D * (cc + 1)], y[:, b, t, P * cc:P * (cc + 1)],
                                                wp_g[:, b, t, :], start=t == 0, stop=t == 1)
                        ins.then_inc(z_made, 1)
                if bb:
                    for b in range(B):
                        pe.wait_ge(f_taken, upto(2 * m + b + 1))
                        wait_over(pe, x2_made, 2 * m + b - 1)
                        for cc in range(2):
                            for k in range(2):
                                ins = pe.matmul(bank[b][1][:, D * cc:D * (cc + 1)], fT[:, b, k, cc, :], w_eff[:, b, k, :],
                                                start=k == 0, stop=k == 1)
                        ins.then_inc(f_made, 1)

            run(pe, turn)


def layer1_attention(nc, sems, keep, aoT, v1):
    ident, h1T, w1T, tri = keep
    with ExitStack() as ctx:
        def sb(name, shape, dt=F32):
            return ctx.enter_context(nc.sbuf_tensor(name, shape, dt))

        def sem(name):
            return sems.enter_context(nc.semaphore(name))

        NT = S // P
        qkT = sb("qkT", [P, B, 2, S])
        p1 = sb("p1", [P, 2, S])
        pT = sb("pT", [P, 2, S])
        mx = sb("mx", [P, 2])
        nm = sb("nm", [P, 2])
        ls = sb("ls", [P, 2])
        rl = sb("rl", [P, 2])
        scores = ctx.enter_context(nc.psum_tensor("scores", [P, S], F32))
        turn_bank = [ctx.enter_context(nc.psum_tensor(f"turn_bank{n}", [P, C], F32)) for n in range(2)]
        out_bank = [ctx.enter_context(nc.psum_tensor(f"out_bank{n}", [P, C], F32)) for n in range(2)]
        banks = [scores[:, C * n:C * (n + 1)] for n in range(4)] + [t[:, :] for t in turn_bank + out_bank]
        filled, taken_a, taken_d = sem("filled"), sem("taken_a"), sem("taken_d")
        scored, masked, maxed, negated, exped, inverted, scaled = (sem("scored"), sem("masked"), sem("maxed"), sem("negated"),
                                                                   sem("exped"), sem("inverted"), sem("scaled"))
        turned, taken, multiplied, ao_taken = sem("turned1"), sem("taken"), sem("multiplied"), sem("ao_taken")

        FILLS = [(b, w, c) for b in range(B) for w in range(3) for c in range(NJ)]
        UNITS = [(b, t) for t in range(NT) for b in range(B)]
        pairs = [-(-(t + 1) // TB) for _, t in UNITS]
        before = [sum(pairs[:u]) for u in range(len(UNITS) + 1)]
        block = ctx.enter_context(nc.Block())

        def into(fill):
            b, w, c = fill
            return qkT[:, b, w, C * c:C * (c + 1)] if w < 2 else v1[:, b, TB * c:TB * (c + 1), :].rearrange("p t d -> p (t d)")

        @block.tensor
        def _(pe):
            for n, (b, w, c) in enumerate(FILLS):
                if n >= 8:
                    pe.wait_ge((taken_a, taken_d)[n % 2], (n - 8) // 2 + 1)
                if w < 2:
                    for k in range(2):
                        ins = pe.matmul(banks[n % 8], w1T[:, k, P * w:P * (w + 1)], h1T[:, b, k, C * c:C * (c + 1)],
                                        start=k == 0, stop=k == 1)
                else:
                    for t in range(TB):
                        for k in range(2):
                            at = C * c + P * t
                            ins = pe.matmul(banks[n % 8][:, P * t:P * (t + 1)], h1T[:, b, k, at:at + P], w1T[:, k, 2 * P:3 * P],
                                            start=k == 0, stop=k == 1)
                ins.then_inc(filled, 1)
            pe.wait_ge(taken_a, len(FILLS) // 2)
            pe.wait_ge(taken_d, len(FILLS) // 2)

            def score(u):
                b, t = UNITS[u]
                if u:
                    pe.wait_ge(exped, u)
                for c in range(pairs[u]):
                    w = min(C, P * (t + 1) - C * c)
                    ins = pe.matmul(scores[:, C * c:C * c + w], qkT[:, b, 0, P * t:P * (t + 1)], qkT[:, b, 1, C * c:C * c + w],
                                    start=True, stop=True)
                ins.then_inc(scored, 1)

            def turn(u, g):
                b, t = UNITS[u]
                n = before[u] + g
                if n >= 2:
                    pe.wait_ge(taken, n - 1)
                for kt in range(TB * g, min(TB * (g + 1), t + 1)):
                    ins = pe.transpose(turn_bank[n % 2][:, P * (kt % TB):P * (kt % TB + 1)], p1[:, u % 2, P * kt:P * (kt + 1)],
                                       ident[:, :])
                ins.then_inc(turned, 1)

            def multiply(u, g):
                b, t = UNITS[u]
                pe.wait_ge(taken, before[u] + g + 1)
                if g == 0 and u >= 2:
                    pe.wait_ge(ao_taken, u - 1)
                for kt in range(TB * g, min(TB * (g + 1), t + 1)):
                    ins = pe.matmul(out_bank[u % 2][:, 0:P], v1[:, b, kt, :], pT[:, u % 2, P * kt:P * (kt + 1)],
                                    start=kt == 0, stop=kt == t)
                ins.then_inc(multiplied, 1)

            for u in range(len(UNITS) + 1):
                if u < len(UNITS):
                    score(u)
                if u:
                    pe.wait_ge(scaled, u)
                    for g in range(pairs[u - 1] + 1):
                        if g < pairs[u - 1]:
                            turn(u - 1, g)
                        if g:
                            multiply(u - 1, g - 1)

        @block.vector
        def _(dve):
            for n in range(1, len(FILLS), 2):
                dve.wait_ge(filled, n + 1)
                dve.tensor_copy(into(FILLS[n]), banks[n % 8]).then_inc(taken_d, 1)

            def normalise(u):
                b, t = UNITS[u]
                dve.wait_ge(exped, u + 1)
                dve.reciprocal(rl[:, u % 2:u % 2 + 1], ls[:, u % 2:u % 2 + 1]).then_inc(inverted, 1)
                dve.wait_ge(inverted, u + 1)
                w = P * (t + 1)
                dve.tensor_scalar(p1[:, u % 2, 0:w], p1[:, u % 2, 0:w], rl[:, u % 2:u % 2 + 1], None, ALU.mult).then_inc(scaled, 1)

            for u, (b, t) in enumerate(UNITS):
                w = P * (t + 1)
                dve.wait_ge(scored, u + 1)
                dve.tensor_tensor(scores[:, w - P:w], scores[:, w - P:w], tri, ALU.add).then_inc(masked, 1)
                dve.wait_ge(masked, u + 1)
                dve.tensor_reduce(mx[:, u % 2:u % 2 + 1], scores[:, 0:w], AX.X, ALU.max).then_inc(maxed, 1)
                dve.wait_ge(maxed, u + 1)
                dve.tensor_scalar(nm[:, u % 2:u % 2 + 1], mx[:, u % 2:u % 2 + 1], -(INNER ** -0.5), None, ALU.mult).then_inc(negated, 1)
                normalise(u)

        @block.scalar
        def _(act):
            for n in range(0, len(FILLS), 2):
                act.wait_ge(filled, n + 1)
                act.activation(into(FILLS[n]), banks[n % 8], ACT.Copy).then_inc(taken_a, 1)

            def take(u):
                b, t = UNITS[u]
                for g in range(pairs[u]):
                    act.wait_ge(turned, before[u] + g + 1)
                    if g == 0 and u >= 2:
                        act.wait_ge(multiplied, before[u - 1])
                    w = min(C, P * (t + 1) - C * g)
                    act.activation(pT[:, u % 2, C * g:C * g + w], turn_bank[(before[u] + g) % 2][:, 0:w], ACT.Copy).then_inc(taken, 1)
                act.wait_ge(multiplied, before[u + 1])
                act.activation(aoT[:, b, :, HD * t:HD * (t + 1)].rearrange("p n c -> p c n"),
                               out_bank[u % 2][:, 0:P].rearrange("p (c n) -> p c n", c=HD), ACT.Copy).then_inc(ao_taken, 1)

            for u, (b, t) in enumerate(UNITS):
                w = P * (t + 1)
                act.wait_ge(negated, u + 1)
                if u >= 2:
                    act.wait_ge(turned, before[u - 1])
                act.activation(p1[:, u % 2, 0:w], scores[:, 0:w], ACT.Exp, bias=nm[:, u % 2:u % 2 + 1], scale=INNER ** -0.5,
                               accum_out=ls[:, u % 2:u % 2 + 1]).then_inc(exped, 1)
                if u:
                    take(u - 1)
            take(len(UNITS) - 1)


def layer1_out(nc, sems, keep, aoT, out):
    rowmod, x2, woT, last_rows = keep
    with ExitStack() as ctx:
        def sb(name, shape, dt=F32):
            return ctx.enter_context(nc.sbuf_tensor(name, shape, dt))

        def sem(name):
            return sems.enter_context(nc.semaphore(name))

        NB = S // ROWS
        one = sb("one", [1, P])
        ao = sb("ao", [P, B, D])
        x3 = sb("x3", [P, B, 2, D])
        x3b = sb("x3b", [P, 2, B, 2, D])
        hn = sb("hn", [P, B, 2, D])
        hs = sb("hs", [P, B, 2, D])
        h2 = sb("h2", [P, B, 2, D])
        yn = sb("yn", [P, B, 2, D])
        yg = sb("yg", [P, B, 2, D])
        st = sb("st3", [P, 2, B, 2, 6])
        mv = sb("mv3", [P, 2, B, 2, 2])
        ve = sb("ve3", [P, 2, B, 2])
        rs = sb("rs3", [P, 2, B, 2])
        half = sb("half3", [P, 2])
        res = sb("res", [P, B, 2, D])
        bank = [ctx.enter_context(nc.psum_tensor(f"o_bank{b}", [P, C], F32)) for b in range(B)]
        consts, staged, projected, x3_made, x3b_made = (sem("consts3"), sem("staged"), sem("projected"), sem("x3_made"),
                                                        sem("x3b_made"))
        ln_step = [[sem(f"s3_{n}{b}") for b in range(B)] for n in range(2)]
        ve_made = [[sem(f"ve3_{n}{b}") for b in range(B)] for n in range(2)]
        rs_made = [[sem(f"rs3_{n}{b}") for b in range(B)] for n in range(2)]
        hn_made, hs_made, h2_made, yn_made, yg_made, res_made, stored = (
            sem("hn_made"), sem("hs_made"), sem("h2_made"), sem("yn_made"), sem("yg_made"), sem("res_made"),
            [sem(f"stored{b}") for b in range(B)])
        block = ctx.enter_context(nc.Block())

        def run(eng, turn):
            turn(0, True, False)
            turn(1, True, True)
            with eng.Fori(2, NB) as n:
                turn(Turns(n), True, True)
            turn(NB, False, True)

        def wait_over(eng, s, count):
            if not (isinstance(count, int) and count <= 0):
                eng.wait_ge(s, upto(count))

        @block.sync
        def _(sp):
            def store(n):
                for b in range(B):
                    sp.wait_ge(res_made, upto(2 * n + b + 1))
                    sp.dma_start(out[b].rearrange("(k c n) d -> c k n d", c=P, n=NB)[:, :, bass.ds(upto(n), 1), :]
                                 .rearrange("c k n d -> c (k n) d"), res[:, b, :, :]).then_inc(stored[b], 16)

            with sp.Fori(0, NB) as n:
                store(Turns(n))
            for b in range(B):
                sp.wait_ge(stored[b], 16 * NB)

        @block.scalar
        def _(act):
            def turn(n, a, bb):
                if a:
                    for b in range(B):
                        wait_over(act, projected, 2 * n + b - 1)
                        act.activation(ao[:, b, :].unsqueeze(1), aoT[:, b, bass.ds(upto(n), 1), :], ACT.Copy).then_inc(staged, 1)

            run(act, turn)

        @block.tensor
        def _(pe):
            pe.wait_ge(consts, 2)

            def turn(n, a, bb):
                if a:
                    for b in range(B):
                        pe.wait_ge(staged, upto(2 * n + b + 1))
                        wait_over(pe, x3_made, 2 * n + b - 1)
                        for k in range(2):
                            cols = bank[b][:, D * k:D * (k + 1)]
                            pe.matmul(cols, ao[:, b, P * k:P * (k + 1)], woT[:, b, :], start=True, stop=False)
                            ins = pe.matmul(cols, one[0:1, :], last_rows[0:1, 0, b, :], start=False, stop=True)
                        ins.then_inc(projected, 1)

            run(pe, turn)

        @block.gpsimd
        def _(pool):
            pool.memset(half[:, :], -0.5).then_inc(consts, 1)
            pool.memset(one[:, :], 1.0).then_inc(consts, 1)
            pool.wait_ge(consts, 2)

            def deviation(n, which, b):
                pool.wait_ge(ve_made[which][b], upto(n + 1))
                pool.tensor_tensor(rs[:, which, b, :], ve[:, which, b, :], half[:, :], ALU.pow).then_inc(rs_made[which][b], 1)

            def turn(n, a, bb):
                m = n - 1
                if bb:
                    for b in range(B):
                        deviation(m, 1, b)
                if a:
                    for b in range(B):
                        deviation(n, 0, b)
                if bb:
                    for b in range(B):
                        pool.wait_ge(yn_made, upto(2 * m + b + 1))
                        wait_over(pool, res_made, 2 * m + b - 1)
                        pool.tensor_tensor(yg[:, b, :, :], yn[:, b, :, :], last_rows[:, 1, b, :].unsqueeze(1).broadcast_to([P, 2, D]),
                                           ALU.mult).then_inc(yg_made, 1)
                if a:
                    for b in range(B):
                        pool.wait_ge(hn_made, upto(2 * n + b + 1))
                        wait_over(pool, h2_made, 2 * n + b - 1)
                        pool.tensor_tensor(hs[:, b, :, :], hn[:, b, :, :], rowmod[:, 4, b, :].unsqueeze(1).broadcast_to([P, 2, D]),
                                           ALU.mult).then_inc(hs_made, 1)

            run(pool, turn)

        @block.vector
        def _(dve):
            def moments(n, which, b, src, made):
                s = ln_step[which][b]
                dve.wait_ge(made, upto(2 * n + b + 1))
                dve.memset(ve[:, which, b, 0:1], EPS).then_inc(s, 1)
                for k in range(2):
                    dve.bn_stats(st[:, which, b, k, :], src(k)).then_inc(s, 1)
                dve.wait_ge(s, upto(6 * n + 3))
                dve.memset(ve[:, which, b, 1:2], EPS).then_inc(s, 1)
                for k in range(2):
                    dve.bn_aggr(mv[:, which, b, k, :], st[:, which, b, k, :]).then_inc(s, 1)
                dve.wait_ge(s, upto(6 * n + 6))
                dve.tensor_tensor(ve[:, which, b, :], mv[:, which, b, :, 1], ve[:, which, b, :], ALU.add) \
                    .then_inc(ve_made[which][b], 1)

            def centre(n, which, b, dst, src, done):
                dve.wait_ge(rs_made[which][b], upto(n + 1))
                for k in range(2):
                    ins = dve.tensor_scalar(dst[:, b, k, :], src[:, b, k, :], mv[:, which, b, k, 0:1], rs[:, which, b, k:k + 1],
                                            ALU.subtract, ALU.mult)
                ins.then_inc(done, 1)

            def turn(n, a, bb):
                m = n - 1
                if bb:
                    for b in range(B):
                        dve.wait_ge(hs_made, upto(2 * m + b + 1))
                        wait_over(dve, yn_made, 2 * m + b - 1)
                        dve.tensor_tensor(h2[:, b, :, :], hs[:, b, :, :], rowmod[:, 3, b, :].unsqueeze(1).broadcast_to([P, 2, D]),
                                          ALU.add).then_inc(h2_made, 1)
                        moments(m, 1, b, lambda k: h2[:, b, k, :], h2_made)
                        wait_over(dve, res_made, 2 * m + b - 1)
                        dve.tensor_tensor(x3b[:, 0, b, :, :], x3[:, b, :, :], last_rows[:, 2, b, :].unsqueeze(1).broadcast_to([P, 2, D]),
                                          ALU.add).then_inc(x3b_made, 1)
                if a:
                    for b in range(B):
                        dve.wait_ge(projected, upto(2 * n + b + 1))
                        wait_over(dve, x3b_made, 2 * n + b - 1)
                        dve.tensor_tensor(x3[:, b, :, :], bank[b][:, :].rearrange("p (k d) -> p k d", k=2),
                                          x2[:, bass.ds(upto(n), 1), b, :, :].rearrange("p m k d -> p (m k) d"), ALU.add) \
                            .then_inc(x3_made, 1)
                        moments(n, 0, b, lambda k: x3[:, b, k, :], x3_made)
                if bb:
                    for b in range(B):
                        centre(m, 1, b, yn, h2, yn_made)
                if a:
                    for b in range(B):
                        wait_over(dve, hs_made, 2 * n + b - 1)
                        centre(n, 0, b, hn, x3, hn_made)
                if bb:
                    for b in range(B):
                        dve.wait_ge(yg_made, upto(2 * m + b + 1))
                        wait_over(dve, stored[b], 16 * m)
                        dve.wait_ge(x3b_made, upto(2 * m + b + 1))
                        dve.tensor_tensor(res[:, b, :, :], x3b[:, 0, b, :, :], yg[:, b, :, :], ALU.add).then_inc(res_made, 1)

            run(dve, turn)


def adaln_kernel(nc, x, Wqkv, Wproj, lq1, lk1, lq2, lk2, fW, fb, fV, fC, c0, wmod0, w_qkv, w_out, b_out,
                 ln_g, ln_b, c1, wmod1, out):
    with ExitStack() as sems, ExitStack() as ctx:
        def sb(name, shape):
            return ctx.enter_context(nc.sbuf_tensor(name, shape, F32))

        ident = sb("ident", [P, P])
        mask_a = sb("mask_a", [P, C])
        colmod = sb("colmod", [P, 6, 2, B])
        rowmod = sb("rowmod", [P, 6, B, D])
        attn = sb("attn", [P, GROUPS, S // P, 2 * HD])
        layer0_attention(nc, sems, (ident, mask_a, colmod, rowmod, attn), x, Wqkv, lq1, lk1, lq2, lk2, c0, wmod0, c1, wmod1)

        x2 = sb("x2", [P, KV, B, 2, D])
        h1T = sb("h1T", [P, B, 2, S])
        w1T = sb("w1T", [P, 2, 3 * INNER])
        woT = sb("woT", [P, B, D])
        last_rows = sb("last_rows", [P, 3, B, D])
        layer0_out(nc, sems, (ident, colmod, rowmod, attn, x2, h1T, w1T, woT, last_rows), x, Wproj, fW, fb, fV, fC, w_qkv,
                   w_out, b_out, ln_g, ln_b)

        free = attn[:, :, :, :].rearrange("p g t e -> p (g t e)")
        aoT = free[:, 0:B * S].rearrange("p (b n c) -> p b n c", b=B, n=KV)
        v1 = free[:, B * S:2 * B * S].rearrange("p (b t d) -> p b t d", b=B, t=S // P)
        layer1_attention(nc, sems, (ident, h1T, w1T, mask_a[:, C - P:C]), aoT, v1)
        layer1_out(nc, sems, (rowmod, x2, woT, last_rows), aoT, out)


_INS = ["L0_attn_x", "L0_attn_Wqkv", "L0_attn_Wproj", "L0_attn_lambda_q1", "L0_attn_lambda_k1", "L0_attn_lambda_q2",
        "L0_attn_lambda_k2", "L0_ffn_W", "L0_ffn_b", "L0_ffn_V_r", "L0_ffn_C", "L0_c", "L0_wmod", "L1_attn_w_qkv",
        "L1_attn_w_out", "L1_attn_b_out", "L1_ffn_ln_g", "L1_ffn_ln_b", "L1_c", "L1_wmod"]


def kernel(**inputs):
    import concourse.bacc as bacc
    from concourse.bass_utils import run_bass_kernel_spmd

    nc = bacc.Bacc("TRN2", target_bir_lowering=False, num_devices=1)
    arrays, args = {}, []
    for name in _INS:
        a = np.ascontiguousarray(inputs[name])
        arrays[f"in_{name}"] = a
        args.append(nc.dram_tensor(f"in_{name}", a.shape, mybir.dt.from_np(a.dtype), kind="ExternalInput").ap())
    out = nc.dram_tensor("out_0", (B, S, D), F32, kind="ExternalOutput").ap()
    adaln_kernel(nc, *args, out)
    r = run_bass_kernel_spmd(nc, [arrays], core_ids=[0])
    return r.results[0]["out_0"]
```

```python
import math
from contextlib import ExitStack

import numpy as np

import concourse.bass as bass
from concourse import mybir

ALU = mybir.AluOpType
ACT = mybir.ActivationFunctionType
AX = mybir.AxisListType
F32 = mybir.dt.float32
BF16 = mybir.dt.bfloat16

P = 128
B, S, D = 2, 2048, 256
HD = 16
KV = 8
QH = 4
GROUPS = B * KV
ROWS = S // KV
C = 512
NJ = S // C
TB = C // P
PARTS_Q = (0, 0, 1, 1, 0, 2)
PARTS_K = (0, 1, 0, 1, 2, 0)
KP_ROWS = HD * len(PARTS_Q)
KP_ALL = KP_ROWS + 2
NEG = -3.0e38
EPS = 1e-5
LAMBDA_INIT = 0.8 - 0.6 * math.exp(-0.3)
INNER = 128

B_STEPS = [(j, pieces) for j in range(NJ)
           for pieces in [[(kt, 0, 0)] for kt in range(TB * j + 1)]
           + [[(TB * j + 1, P, P), (TB * j + 3, 0, 3 * P)], [(TB * j + 2, 2 * P, 2 * P)]]]
STEPS = len(B_STEPS)
J_FIRST = [min(s for s in range(STEPS) if B_STEPS[s][0] == j) for j in range(NJ)]
J_LAST = [max(s for s in range(STEPS) if B_STEPS[s][0] == j) for j in range(NJ)]
DIAG = [s for s, (j, pieces) in enumerate(B_STEPS) if pieces[0][0] >= TB * j]
A_UNITS = [(j, t, c, hp) for j in range(NJ) for t in range(TB) for c in range(j + 1) for hp in range(QH // 2)]
UNITS = len(A_UNITS)
A_RING = 2
B_RING = 3
P_RING = 3
LAG = 2


def widths(s):
    return [C - q for _, _, q in B_STEPS[s][1]]


def first_col(s):
    return min(at for _, at, _ in B_STEPS[s][1])


def width_a(u):
    j, t, c, _ = A_UNITS[u]
    return P * (t + 1) if c == j else C


LEAD = 46
MET = 1.1
FIXED = 64


def schedule():
    met = [[s - LAG] if s < STEPS - 1 else range(STEPS - 1 - LAG, STEPS) for s in range(STEPS)]
    b_cost = [sum(widths(s)) + (MET * sum(sum(widths(m)) for m in met[s] if m >= 0)) for s in range(STEPS)]
    a_cost = [width_a(u % UNITS) + FIXED for u in range(LEAD, LEAD + UNITS)]
    ends, b_done, a_done, k = [], 0, 0, 0
    for s in range(STEPS):
        b_done += b_cost[s]
        while k < UNITS and a_done + a_cost[k] / 2 < sum(a_cost) * b_done / sum(b_cost):
            a_done += a_cost[k]
            k += 1
        ends.append(k)
    return ends[:-1] + [UNITS]


ENDS = schedule()
A_LAST = [max(u for u in range(UNITS) if A_UNITS[u][0] == j) for j in range(NJ)]


def step_of(u):
    return next(s for s in range(STEPS) if u < ENDS[s])


def units(s):
    return range(LEAD + (ENDS[s - 1] if s else 0), LEAD + ENDS[s])


def share(seq, n, of):
    return seq[len(seq) * n // of:len(seq) * (n + 1) // of]


O_AT = {J_LAST[j] + (3 if j < NJ - 1 else 0): j for j in range(NJ)}
M_AT = {}
for _j in range(NJ):
    _s = step_of((A_LAST[_j] - LEAD) % UNITS) + 1
    M_AT[_s] = _j
NEXT = [j for j in range(NJ) if A_LAST[j] < LEAD]
PREP_AT = {7: "N", 8: "W0", 9: "W1", 10: "W2", 11: "W3", 17: "T0", 18: "T1", 19: "T2", 20: "T3"}
MISC = {s: [n for n in ([f"M{M_AT[s]}"] if s in M_AT else []) + ([f"O{O_AT[s]}"] if s in O_AT else [])
            + ([PREP_AT[s]] if s in PREP_AT else [])] for s in range(STEPS)}
PREP = tuple(PREP_AT.values())


def uses_of(par, last):
    out = []
    for s in range(STEPS):
        for u in MISC.get(s, []):
            if last and (u in PREP or (par == 1 and u in [f"M{j}" for j in NEXT])):
                continue
            out.append((s, u))
    return out


GATES_AT = 24

SLOTS = [slot for par in range(2) for s in range(STEPS)
         for slot in [("B", par, s, h) for h in range(QH)] + [(use, par, s, 0) for use in MISC[s]]]
SLOTS[-1:-1] = [None] * (-len(SLOTS) % B_RING)


def bank_no(slot):
    return SLOTS.index(slot) % B_RING


def occupant(slot, last):
    at = SLOTS.index(slot) - B_RING
    while True:
        was = SLOTS[at % len(SLOTS)]
        if was is not None and (at < 0 or was[0] == "B" or (was[2], was[0]) in uses_of(was[1], last)):
            return was, at < 0
        at -= B_RING


class Turns:

    def __init__(self, i, turns=1, n=0):
        self.i, self.turns, self.n = i, turns, n

    def __add__(self, k):
        return Turns(self.i, self.turns, self.n + k)

    def __sub__(self, k):
        return self + -k

    def __mul__(self, k):
        return Turns(self.i, self.turns * k, self.n * k)

    __radd__, __rmul__ = __add__, __mul__


def upto(count):
    return count.i * count.turns + count.n if isinstance(count, Turns) else count


def last_use(unit, ring):
    return min(unit + 1, ring)


A_INC = 4
LEAD_TURN = {A_LAST[j] + 4: j for j in NEXT}
HEADS_AT = [min(LEAD_TURN) + 2 + 2 * k for k in range(4)]
PACK_DMAS = (QH + 1) * len(PARTS_Q)
START = 1
POOL_CONSTS = 13
ROW_MODS = [(0, 0, (2, 5), 0), (0, 1, (2, 5), 0), (1, 0, (2, 3), 2), (1, 0, (4, 5), 4), (1, 1, (2, 3), 2), (1, 1, (4, 5), 4)]


def layer0_attention(nc, sems, keep, x, Wqkv, lq1, lk1, lq2, lk2, c0, wmod0, c1, wmod1):
    ident, mask_a, colmod, rowmod, attn = keep
    with ExitStack() as ctx:
        def sb(name, shape, dt=F32):
            return ctx.enter_context(nc.sbuf_tensor(name, shape, dt))

        def ps(name, shape, dt=F32):
            return ctx.enter_context(nc.psum_tensor(name, shape, dt))

        def sem(name):
            return sems.enter_context(nc.semaphore(name))

        identb = sb("identb", [P, P], BF16)
        cmod = sb("cmod", [P, 2, 2, GROUPS])
        signs = sb("signs", [P, TB, QH])
        starts = sb("starts", [P, 4])
        expo = sb("expo", [P, 8])
        wqkv = sb("wqkv", [P, 2, 3 * D])
        q_pack = [sb(f"q_pack{i}", [P, QH, S], BF16) for i in range(2)]
        k_pack = [sb(f"k_pack{i}", [P, S], BF16) for i in range(2)]
        v_tile = [sb(f"v_tile{i}", [P, S // P, 32]) for i in range(2)]
        probs = sb("probs", [P, P_RING, QH, C])
        xg = sb("xg", [P, 2, D])
        xhat = sb("xhat", [P, 2, D])
        stats = sb("stats", [P, 2, 6])
        mv = sb("mv", [P, 2, 2])
        veps = sb("veps", [P, 2])
        rstd = sb("rstd", [P, 2])
        hT = sb("hT", [P, 2, ROWS])
        qkv_row = sb("qkv_row", [P, 2, 3 * D])
        heads = sb("heads", [P, QH + 1, D])
        heads_by_j = sb("heads_by_j", [P, D // HD, QH + 1, HD])
        headT = sb("headT", [P, S])
        rest = sb("rest", [P, S])
        part = [sb(f"part{i}", [P, S], BF16) for i in range(3)]
        m_part = sb("m_part", [P, QH, TB, NJ])
        m_max = sb("m_max", [P, QH, TB])
        m_neg = sb("m_neg", [P, QH, 2, TB], BF16)
        m_rows = sb("m_rows", [32, P], BF16)
        o_sb = sb("o_sb", [P, C])
        o_rl = sb("o_rl", [P, TB, QH])
        o_w = sb("o_w", [P, TB, QH])
        o_sc = sb("o_sc", [P, 2, TB * QH * HD])
        cT = sb("cT", [P, 2, 2, B])
        cE = sb("cE", [P, 8])
        cS = sb("cS", [P, 2, 2, B])
        cSb = sb("cSb", [P, 2, 2, B, P])
        lam_in = sb("lam_in", [P, 4, P])
        lam = sb("lam", [P, 8])
        wmods = attn[:, :, :, :].rearrange("p g t e -> p (g t e)")[:, 0:6 * D * 4].rearrange(
            "p (l k n) -> p l k n", l=2, k=2)
        gate_t = (headT, rest)

        products = o_sb[:, 0:2 * P].rearrange("p (l n) -> p l n", l=2)

        a_bank = [ps(f"a_bank{i}", [P, 2, C]) for i in range(A_RING)]
        b_bank = [ps(f"b_bank{i}", [P, C]) for i in range(B_RING)]
        acc = ps("acc", [P, C])
        misc = b_bank[B_RING - 1]

        scratch = [nc.dram_tensor(f"scratch{i}", [ROWS * 3 * D], F32, kind="Internal").ap() for i in range(2)]

        pool_consts, dve_consts, act_consts = sem("pool_consts"), sem("dve_consts"), sem("act_consts")
        mod_ready, mod_taken = sem("mod_ready"), sem("mod_taken")
        cT_in, wmod_a_in, wmod_b_in, wqkv_in, lam_inputs = (sem("cT_in"), sem("wmod_a_in"), sem("wmod_b_in"), sem("wqkv_in"),
                                                           sem("lam_inputs"))
        silu_ready, cmod_ready, gate_step, lam_step = sem("silu_ready"), sem("cmod_ready"), sem("gate_step"), sem("lam_step")
        ln_step, m_step, o_step = sem("ln_step"), sem("m_step"), sem("o_step")
        x_loaded, stats_ready, rstd_ready, xhat_ready = sem("x_loaded"), sem("stats_ready"), sem("rstd_ready"), sem("xhat_ready")
        misc_filled = sem("misc_filled")
        hT_ready, rows_ready, rows_out, heads_in, v_in = (sem("hT_ready"), sem("rows_ready"), sem("rows_out"),
                                                          sem("heads_in"), [sem(f"v_in{i}") for i in range(2)])
        heads_ready = sem("heads_ready")
        turned, part0_ready, rest_ready, parts_ready, packs_in = (sem("turned"), sem("part0_ready"), sem("rest_ready"),
                                                                 sem("parts_ready"), sem("packs_in"))
        a_scored, a_maxed, m_ready, m_copied, m_rows_in = (sem("a_scored"), sem("a_maxed"), sem("m_ready"),
                                                          sem("m_copied"), sem("m_rows_in"))
        b_scored, b_exped, b_masked, pv_done = sem("b_scored"), sem("b_exped"), sem("b_masked"), sem("pv_done")
        acc_copied, o_scaled, o_added = sem("acc_copied"), sem("o_scaled"), sem("o_added")
        dve_step = sem("dve_step")

        N_PRO = 20
        PER = 2 * 17

        def a_count(i, par, u):
            return 2 * UNITS * i + UNITS * par + u

        def block_no(g, j):
            return 4 * g + j + (NJ if j in NEXT else 0)

        def misc_no(i, par, last, s, name):
            n = N_PRO + 1 + (len(uses_of(0, last)) if par else 0) + uses_of(par, last).index((s, name))
            return PER * i + n

        def regions(buf):
            n = ROWS * 2 * D
            return scratch[buf][0:n], scratch[buf][n:n + ROWS * P], scratch[buf][n + ROWS * P:]

        block = ctx.enter_context(nc.Block())

        x_rows = x.rearrange("b s d -> (b s) d")

        @block.sync
        def _(sp):
            for layer, c in enumerate((c0, c1)):
                for n in range(B):
                    sp.dma_start(cT[:, layer, :, n], c[n, :].rearrange("(k p) -> p k", p=P),
                                 allow_slow_non_contiguous=True).then_inc(cT_in, 16)

            def load_x(n, unused):
                if unused is not None:
                    sp.wait_ge(xhat_ready, upto(unused))
                sp.dma_start(xg[:, :, :], x_rows[bass.ds(upto(n * ROWS), ROWS), :].rearrange("(r p) d -> p r d", p=P)) \
                    .then_inc(x_loaded, 16)

            load_x(0, None)
            sp.dma_start(wmods[:, 0, :, 0:2 * D], wmod0.rearrange("(k p) n -> p k n", p=P)[:, :, 0:2 * D]).then_inc(wmod_a_in, 16)
            sp.dma_start(wqkv[:, :, :], Wqkv.rearrange("(k p) n -> p k n", p=P)).then_inc(wqkv_in, 16)
            load_x(1, 1)
            sp.dma_start(wmods[:, 0, :, 2 * D:6 * D], wmod0.rearrange("(k p) n -> p k n", p=P)[:, :, 2 * D:6 * D]).then_inc(wmod_b_in, 16)
            sp.dma_start(wmods[:, 1, :, :], wmod1.rearrange("(k p) n -> p k n", p=P)).then_inc(wmod_b_in, 16)
            for k, v in enumerate((lq1, lk1, lq2, lk2)):
                sp.dma_start(lam_in[:, k, :], v.rearrange("(o n) -> o n", o=1).broadcast_to([P, P])).then_inc(lam_inputs, 16)

            def rows_to_dram(n, buf):
                sp.wait_ge(rows_ready, upto(4 * (n + 1)))
                q, k, v = regions(buf)
                for reg, cols in ((q, slice(0, 2 * D)), (k, slice(2 * D, 2 * D + P)), (v, slice(2 * D + P, 3 * D))):
                    sp.dma_start(reg.rearrange("(r p e) -> p r e", r=2, p=P), qkv_row[:, :, cols]).then_inc(rows_out, 16)

            def heads_from_dram(n, buf, gathered):
                sp.wait_ge(rows_out, upto(48 * (n + 1)))
                if gathered is not None:
                    sp.wait_ge(heads_ready, gathered)
                q, k, _ = regions(buf)
                sp.dma_start(heads[:, 0:QH, :], q.rearrange("(h p e) -> p h e", h=QH, p=P)).then_inc(heads_in, 16)
                sp.dma_start(heads[:, QH, :], k.rearrange("(p e) -> p e", p=P)).then_inc(heads_in, 16)

            def pack(n, buf, steps_done):
                if steps_done is not None:
                    sp.wait_ge(pv_done, upto(START + steps_done))
                    sp.wait_ge(parts_ready, upto(n + 1))
                for p in range(3):
                    if steps_done is None:
                        sp.wait_ge(*((part0_ready, 1), (rest_ready, 2), (parts_ready, 1))[p])
                    for r, (pq, pk) in enumerate(zip(PARTS_Q, PARTS_K)):
                        if pk == p:
                            sp.dma_start(k_pack[buf][HD * r:HD * (r + 1), :], part[p][HD * QH:HD * (QH + 1), :]).then_inc(packs_in, 16)
                        for h in range(QH if pq == p else 0):
                            sp.dma_start(q_pack[buf][HD * r:HD * (r + 1), h, :], part[p][HD * h:HD * (h + 1), :]).then_inc(packs_in, 16)
                sp.dma_start(v_tile[buf][:, :, 0:HD], regions(buf)[2].rearrange("(t p d) -> p t d", p=P, d=HD)).then_inc(v_in[buf], 16)

            def maxima_rows(count, buf, j):
                sp.wait_ge(m_copied, upto(count))
                for h in range(QH):
                    sp.dma_start(q_pack[buf][KP_ROWS:KP_ALL, h, C * j:C * (j + 1)], m_rows[2 * TB * h:2 * TB * (h + 1), :]) \
                        .then_inc(m_rows_in, 16)

            rows_to_dram(0, 0)
            heads_from_dram(0, 0, None)
            rows_to_dram(1, 1)
            heads_from_dram(1, 1, 1)
            sp.wait_ge(pool_consts, POOL_CONSTS)
            pack(0, 0, None)
            maxima_rows(1, 0, 0)
            maxima_rows(2, 0, 1)

            def body(i, last):
                for par in range(2):
                    g = 2 * i + par
                    if not last:
                        load_x(g + 2, g + 2)
                    if not (last and par == 1):
                        pack(g + 1, 1 - par, STEPS * g)
                    maxima_rows(4 * g + 3, par, 2)
                    if not last:
                        rows_to_dram(g + 2, par)
                        heads_from_dram(g + 2, par, None)
                    maxima_rows(4 * g + 4, par, 3)
                    if not (last and par == 1):
                        maxima_rows(4 * g + 5, 1 - par, 0)
                        maxima_rows(4 * g + 6, 1 - par, 1)

            with sp.Fori(0, GROUPS // 2 - 1) as i:
                body(Turns(i), False)
            body(GROUPS // 2 - 1, True)

        @block.gpsimd
        def _(pool):
            def made(ins):
                return ins.then_inc(pool_consts, 1)

            pool.memset(starts[:, 0:1], 0.0).then_inc(o_added, START)
            made(pool.memset(ident[:, :], 0.0))
            made(pool.memset(identb[:, :], 0.0))
            made(pool.memset(mask_a[:, :], 0.0))
            made(pool.memset(expo[:, :], -0.5))
            pool.wait_ge(pool_consts, 4)
            for m in (ident, identb):
                made(pool.affine_select(out=m[:, :], in_=m[:, :], compare_op=ALU.not_equal, fill=1.0, base=0,
                                        pattern=[[-1, P]], channel_multiplier=1))
            made(pool.affine_select(out=mask_a[:, C - P:C], in_=mask_a[:, C - P:C], compare_op=ALU.is_ge, fill=NEG, base=0,
                                    pattern=[[-1, P]], channel_multiplier=1))
            for buf in range(2):
                made(pool.memset(v_tile[buf][:, :, HD:32], 0.0))
            pool.wait_ge(pool_consts, 9)
            for buf in range(2):
                made(pool.memset(k_pack[buf][KP_ROWS:P, :], 1.0))
            pool.wait_ge(pool_consts, 11)
            for buf in range(2):
                made(pool.memset(v_tile[buf][:, :, HD:HD + 1], 1.0))

            def inverse_deviation(n):
                pool.wait_ge(stats_ready, upto(n + 1))
                if not (isinstance(n, int) and n == 0):
                    pool.wait_ge(xhat_ready, upto(n))
                pool.tensor_tensor(rstd[:, :], veps[:, :], expo[:, 0:2], ALU.pow).then_inc(rstd_ready, 1)

            def split(n):
                pool.wait_ge(part0_ready, upto(n + 1))
                if not (isinstance(n, int) and n == 0):
                    pool.wait_ge(packs_in, upto(16 * PACK_DMAS * n))
                pool.tensor_tensor(rest[0:80, :], headT[0:80, :], part[0][0:80, :], ALU.subtract).then_inc(rest_ready, 1)
                pool.tensor_tensor(part[1][0:80, :], headT[0:80, :], part[0][0:80, :], ALU.subtract).then_inc(rest_ready, 1)
                pool.wait_ge(rest_ready, upto(2 * (n + 1)))
                pool.tensor_tensor(part[2][0:80, :], rest[0:80, :], part[1][0:80, :], ALU.subtract).then_inc(parts_ready, 1)

            inverse_deviation(0)
            inverse_deviation(1)
            split(1)

            def mask(i, par, s):
                at, blocks = first_col(s) if len(widths(s)) == 1 else 0, len(widths(s))
                blk = probs[:, s % P_RING, :, at:at + P * blocks]
                if blocks > 1:
                    blk = blk.rearrange("p h (a q) -> p h a q", a=blocks)
                pool.wait_ge(b_exped, upto(START + 8 * STEPS * i + 4 * (STEPS * par + s) + 4))
                pool.affine_select(out=blk, in_=blk, compare_op=ALU.is_ge, fill=0.0, base=0,
                                   pattern=[[0, QH]] + [[0, blocks]] * (blocks > 1) + [[1, P]],
                                   channel_multiplier=-1).then_inc(b_masked, 2)

            def pair(i, par, j):
                n = 4 * (2 * i + par) + j
                o = o_sc[:, j % 2, :].rearrange("p (t a c e) -> p t a c e", t=TB, a=2, c=2)
                dst = attn[:, bass.ds(upto(2 * i + par), 1), TB * j:TB * (j + 1), :].rearrange("p g t (a e) -> p (g t) a e", a=2)
                pool.wait_ge(o_scaled, upto(START + n + 1))
                pool.tensor_tensor(dst, o[:, :, :, 0, :], o[:, :, :, 1, :], ALU.add).then_inc(o_added, 1)

            def body(i, last):
                for par in range(2):
                    for s in range(STEPS):
                        if s in DIAG:
                            mask(i, par, s)
                        if s == 3 and not last:
                            inverse_deviation(2 * i + par + 2)
                        if s in O_AT:
                            pair(i, par, O_AT[s])
                        if s == 22 and not last:
                            split(2 * i + par + 2)

            with pool.Fori(0, GROUPS // 2 - 1) as i:
                body(Turns(i), False)
            body(GROUPS // 2 - 1, True)

        @block.vector
        def _(dve):
            dve.memset(starts[:, 1:2], 0.0).then_inc(o_scaled, START)
            dve.wait_ge(act_consts, 1)
            dve.tensor_scalar(cE[:, :], cE[:, :], 1.0, None, ALU.add).then_inc(dve_step, 1)
            dve.wait_ge(dve_step, 1)
            dve.reciprocal(cE[:, :], cE[:, :]).then_inc(dve_step, 1)
            dve.wait_ge(dve_step, 2)
            dve.tensor_tensor(cS[:, :, :, :].rearrange("p l k b -> p (l k b)"), cT[:, :, :, :].rearrange("p l k b -> p (l k b)"),
                              cE[:, :], ALU.mult).then_inc(dve_step, 1)
            dve.wait_ge(dve_step, 3)
            dve.tensor_copy(cSb[:, :, :, :, :].rearrange("p l k b n -> p (l k b) n"),
                            cS[:, :, :, :].rearrange("p l k b -> p (l k b)").unsqueeze(2).broadcast_to([P, 8, P])) \
                .then_inc(silu_ready, 1)

            def normalise(n):
                dve.wait_ge(x_loaded, upto(16 * (n + 1)))
                for r in range(2):
                    dve.bn_stats(stats[:, r, :], xg[:, r, :]).then_inc(ln_step, 1)
                dve.wait_ge(ln_step, upto(5 * n + 2))
                dve.memset(veps[:, :], EPS).then_inc(ln_step, 1)
                for r in range(2):
                    dve.bn_aggr(mv[:, r, :], stats[:, r, :]).then_inc(ln_step, 1)
                dve.wait_ge(ln_step, upto(5 * n + 5))
                dve.tensor_tensor(veps[:, :], mv[:, :, 1], veps[:, :], ALU.add).then_inc(stats_ready, 1)

            def centre(n):
                dve.wait_ge(rstd_ready, upto(n + 1))
                if not (isinstance(n, int) and n == 0):
                    dve.wait_ge(hT_ready, upto(2 * n))
                dve.tensor_scalar(xhat[:, 0, :], xg[:, 0, :], mv[:, 0, 0:1], rstd[:, 0:1], ALU.subtract, ALU.mult)
                dve.tensor_scalar(xhat[:, 1, :], xg[:, 1, :], mv[:, 1, 0:1], rstd[:, 1:2], ALU.subtract, ALU.mult) \
                    .then_inc(xhat_ready, 1)

            def gather_heads(n):
                dve.wait_ge(heads_in, upto(32 * (n + 1)))
                if not (isinstance(n, int) and n == 0):
                    dve.wait_ge(turned, upto(4 * n))
                dve.tensor_copy(heads_by_j[:, :, :, :], heads[:, :, :].rearrange("p h (j d) -> p j h d", d=HD)) \
                    .then_inc(heads_ready, 1)

            normalise(0)
            centre(0)
            dve.wait_ge(mod_ready, 1)
            dve.tensor_copy(colmod[:, 0, :, :], b_bank[0][:, 0:4].rearrange("p (k b) -> p k b", k=2)).then_inc(dve_step, 1)
            dve.tensor_scalar(colmod[:, 1, :, :], b_bank[0][:, 4:8].rearrange("p (k b) -> p k b", k=2), 1.0, None, ALU.add) \
                .then_inc(dve_step, 1)
            dve.wait_ge(dve_step, 5)
            for w in range(2):
                ins = dve.tensor_copy(cmod[:, w, :, :].rearrange("p k (b g) -> p (k b) g", b=B),
                                      colmod[:, w, :, :].rearrange("p k b -> p (k b)").unsqueeze(2).broadcast_to([P, 2 * B, KV]))
                ins.then_inc(cmod_ready, 1)
            normalise(1)
            centre(1)
            gather_heads(0)
            dve.wait_ge(part0_ready, 1)
            dve.tensor_tensor(rest[0:80, :], headT[0:80, :], part[0][0:80, :], ALU.subtract).then_inc(rest_ready, 1)
            dve.tensor_tensor(part[1][0:80, :], headT[0:80, :], part[0][0:80, :], ALU.subtract).then_inc(rest_ready, 1)
            dve.wait_ge(rest_ready, 2)
            dve.tensor_tensor(part[2][0:80, :], rest[0:80, :], part[1][0:80, :], ALU.subtract).then_inc(parts_ready, 1)
            dve.wait_ge(mod_ready, 2)
            for w in range(2, 6):
                src = b_bank[1][:, 4 * (w - 2):4 * (w - 1)].rearrange("p (k b) -> p k b", k=2)
                if w % 2:
                    dve.tensor_scalar(colmod[:, w, :, :], src, 1.0, None, ALU.add).then_inc(dve_step, 1)
                else:
                    dve.tensor_copy(colmod[:, w, :, :], src).then_inc(dve_step, 1)
            for n in range(6):
                dve.wait_ge(mod_ready, upto(3 + n))
                _, b, _, at = ROW_MODS[n]
                dve.tensor_copy(rowmod[:, at:at + 2, b, :],
                                (b_bank[0], acc)[n % 2][:, :].rearrange("p (w d) -> p w d", w=2)).then_inc(mod_taken, 1)
            dve.wait_ge(lam_inputs, 64)
            dve.tensor_tensor(products, lam_in[:, 0:4:2, :], lam_in[:, 1:4:2, :], ALU.mult).then_inc(lam_step, 1)
            dve.wait_ge(lam_step, 1)
            dve.tensor_reduce(lam[:, 0:2], products, AX.X, ALU.add).then_inc(lam_step, 1)
            dve.wait_ge(act_consts, 2)
            dve.tensor_tensor(lam[:, 4:5], lam[:, 3:4], lam[:, 2:3], ALU.subtract).then_inc(lam_step, 1)
            dve.wait_ge(lam_step, 3)
            dve.tensor_scalar(lam[:, 5:6], lam[:, 4:5], -LAMBDA_INIT, 1.0 - LAMBDA_INIT, ALU.add, ALU.mult).then_inc(lam_step, 1)
            dve.memset(lam[:, 6:7], 1.0 - LAMBDA_INIT).then_inc(lam_step, 1)
            dve.wait_ge(lam_step, 5)
            dve.tensor_copy(signs[:, :, 0:4:2], lam[:, 6:7].unsqueeze(1).broadcast_to([P, TB, 2])).then_inc(lam_step, 1)
            dve.tensor_copy(signs[:, :, 1:4:2], lam[:, 5:6].unsqueeze(1).broadcast_to([P, TB, 2])).then_inc(lam_step, 1)
            dve.wait_ge(pool_consts, POOL_CONSTS)
            gather_heads(1)

            def maximum(i, par, u):
                j, t, c, hp = A_UNITS[u % UNITS]
                w, bank = width_a(u % UNITS), a_bank[(UNITS * par + u) % A_RING]
                dve.wait_ge(a_scored, upto(a_count(i, par, u) + 1))
                if c == j:
                    for k in range(2):
                        dve.tensor_tensor_reduce(out=bank[:, k, 0:w], in0=bank[:, k, 0:w], in1=mask_a[:, C - w:C], scale=1.0,
                                                 scalar=NEG, op0=ALU.add, op1=ALU.max,
                                                 accum_out=m_part[:, 2 * hp + k, t, c:c + 1]).then_inc(a_maxed, A_INC // 2)
                else:
                    dve.tensor_reduce(m_part[:, 2 * hp:2 * hp + 2, t, c], bank[:, :, 0:w], AX.X, ALU.max).then_inc(a_maxed, A_INC)

            def negate(i, par, u, j, m):
                dve.wait_ge(a_maxed, upto(A_INC * (a_count(i, par, u) + 1)))
                dve.tensor_reduce(m_max[:, :, :], m_part[:, :, :, 0:j + 1], AX.X, ALU.max).then_inc(m_step, 1)
                dve.wait_ge(m_step, upto(2 * m + 1))
                if not (isinstance(m, int) and m == 0):
                    dve.wait_ge(m_copied, upto(m))
                dve.tensor_scalar(m_neg[:, :, 0, :], m_max[:, :, :], -1.0, None, ALU.mult).then_inc(m_step, 1)
                dve.wait_ge(m_step, upto(2 * m + 2))
                dve.scalar_tensor_tensor(out=m_neg[:, :, 1, :], in0=m_max[:, :, :], scalar=-1.0, in1=m_neg[:, :, 0, :],
                                         op0=ALU.mult, op1=ALU.subtract).then_inc(m_ready, 1)

            def weigh(i, par, last, s, j):
                n = 4 * (2 * i + par) + j
                o = b_bank[bank_no((f"O{j}", par, s, 0))][:, :].rearrange("p (t h e) -> p t h e", t=TB, h=QH)
                dve.wait_ge(misc_filled, upto(misc_no(i, par, last, s, f"O{j}")))
                dve.reciprocal(o_rl[:, :, :], o[:, :, :, HD]).then_inc(o_step, 1)
                dve.wait_ge(o_step, upto(2 * n + 1))
                dve.tensor_tensor(o_w[:, :, :], o_rl[:, :, :], signs[:, :, :], ALU.mult).then_inc(o_step, 1)
                dve.wait_ge(o_step, upto(2 * n + 2))
                dve.wait_ge(o_added, upto(START + n - (1 if par or j else 0)))
                dve.tensor_tensor(o_sc[:, j % 2, :].rearrange("p (t h e) -> p t h e", t=TB, h=QH), o[:, :, :, 0:HD],
                                  o_w[:, :, :].unsqueeze(3).broadcast_to([P, TB, QH, HD]), ALU.mult).then_inc(o_scaled, 1)

            for u in range(LEAD):
                maximum(0, 0, u)
                if u in A_LAST:
                    negate(0, 0, u, A_LAST.index(u), A_LAST.index(u))

            def gates():
                dve.wait_ge(parts_ready, GROUPS)
                dve.wait_ge(mod_taken, 6)
                for n, w in enumerate((0, 1, 2, 5)):
                    g = rowmod[:, w, :, :].rearrange("p b d -> p (b d)")
                    t, u = gate_t[0][:, 0:2 * D], gate_t[1][:, 0:2 * D]
                    if n:
                        dve.wait_ge(gate_step, 4 * n)
                    dve.scalar_tensor_tensor(out=t, in0=g, scalar=-1.0, in1=g, op0=ALU.mult, op1=ALU.max).then_inc(gate_step, 1)
                    dve.tensor_scalar(u, g, 0.0, 2.0, ALU.is_ge, ALU.mult).then_inc(gate_step, 1)
                    dve.wait_ge(gate_step, 4 * n + 1)
                    dve.tensor_scalar(t, t, 0.25, None, ALU.max).then_inc(gate_step, 1)
                    dve.wait_ge(gate_step, 4 * n + 3)
                    dve.scalar_tensor_tensor(out=g, in0=u, scalar=-1.0, in1=t, op0=ALU.add, op1=ALU.mult).then_inc(gate_step, 1)
                dve.tensor_scalar(rowmod[:, 4, :, :], rowmod[:, 4, :, :], 1.0, None, ALU.add)

            def body(i, last):
                for par in range(2):
                    g = 2 * i + par
                    for s in range(STEPS):
                        for u in units(s):
                            if last and par == 1 and u >= UNITS:
                                break
                            maximum(i, par, u)
                            if u % UNITS in A_LAST:
                                j = A_LAST.index(u % UNITS)
                                negate(i, par, u, j, block_no(g, j))
                        if s in O_AT:
                            weigh(i, par, last, s, O_AT[s])
                        if last and par == 1 and s == GATES_AT:
                            gates()
                        if not last and s == 1:
                            normalise(g + 2)
                        if not last and s == 5:
                            centre(g + 2)
                        if not last and s == 15:
                            gather_heads(g + 2)

            with dve.Fori(0, GROUPS // 2 - 1) as i:
                body(Turns(i), False)
            body(GROUPS // 2 - 1, True)

        @block.scalar
        def _(act):
            act.wait_ge(cT_in, 64)
            act.activation(starts[:, 2:3], cT[:, 0, 0, 0:1], ACT.Copy).then_inc(b_exped, START)
            act.activation(starts[:, 3:4], cT[:, 0, 0, 0:1], ACT.Copy).then_inc(acc_copied, START)
            act.activation(cE[:, :], cT[:, :, :, :].rearrange("p l k b -> p (l k b)"), ACT.Exp, scale=-1.0).then_inc(act_consts, 1)

            def shift_rows(n, no, misc=misc):
                act.wait_ge(misc_filled, upto(no))
                if isinstance(n, int) and n == 0:
                    act.wait_ge(cmod_ready, 2)
                for k in range(2):
                    ins = act.activation(hT[:, k, :], misc[:, 2 * P * k:2 * P * (k + 1)], ACT.Identity,
                                         bias=cmod[:, 0, k, bass.ds(upto(n), 1)], scale=cmod[:, 1, k, bass.ds(upto(n), 1)])
                    ins.then_inc(hT_ready, 1)

            def take_rows(n, w, no, misc=misc):
                r, (a, b) = w // 2, ((0, 2 * D), (2 * D, 3 * D))[w % 2]
                if w == 0 and not (isinstance(n, int) and n == 0):
                    act.wait_ge(rows_out, upto(48 * n))
                act.wait_ge(misc_filled, upto(no))
                act.activation(qkv_row[:, r, a:b], misc[:, 0:b - a], ACT.Copy).then_inc(rows_ready, 1)

            def take_heads(n, k, no, misc=misc):
                if k == 0 and not (isinstance(n, int) and n == 0):
                    act.wait_ge(parts_ready, upto(n))
                act.wait_ge(misc_filled, upto(no))
                act.activation(headT[0:80, :].rearrange("q (p j) -> q j p", j=16)[:, 4 * k:4 * (k + 1), :],
                               misc[0:80, :].rearrange("q (j p) -> q j p", j=4), ACT.Copy).then_inc(turned, 1)

            def first_part(n):
                act.wait_ge(turned, upto(4 * (n + 1)))
                if not (isinstance(n, int) and n == 0):
                    act.wait_ge(packs_in, upto(16 * PACK_DMAS * n))
                act.activation(part[0][0:80, :], headT[0:80, :], ACT.Copy).then_inc(part0_ready, 1)

            def take_maxima(m, no, misc=misc):
                act.wait_ge(misc_filled, upto(no))
                if not (isinstance(m, int) and m == 0):
                    act.wait_ge(m_rows_in, upto(64 * m))
                act.activation(m_rows[:, :], misc[:, :].bitcast(BF16)[0:32, 0:P], ACT.Copy).then_inc(m_copied, 1)

            for n in range(2):
                shift_rows(n, 5 * n + 1)
                for w in range(4):
                    take_rows(n, w, 5 * n + 2 + w)
            for k in range(4):
                take_heads(0, k, 11 + k)
            first_part(0)
            act.wait_ge(lam_step, 2)
            act.activation(lam[:, 2:4], lam[:, 0:2], ACT.Exp).then_inc(act_consts, 1)
            take_maxima(0, 15)
            for k in range(4):
                take_heads(1, k, 16 + k)
            first_part(1)
            take_maxima(1, 20)

            def exponentials(i, par, s):
                at = first_col(s)
                for h in range(QH):
                    unit = 4 * (STEPS * par + s) + h
                    act.wait_ge(b_scored, upto(8 * STEPS * i + unit + 1))
                    if h == 0:
                        act.wait_ge(pv_done, upto(START + 2 * STEPS * i + max(STEPS * par + s - P_RING + 1, 0)))
                    act.activation(probs[:, s % P_RING, h, at:C], b_bank[bank_no(("B", par, s, h))][:, at:C], ACT.Exp, scale=HD ** -0.5) \
                        .then_inc(b_exped, 1)

            def take_output(i, par, j):
                n = 4 * (2 * i + par) + j
                act.wait_ge(pv_done, upto(START + 2 * STEPS * i + STEPS * par + J_LAST[j] + 1))
                act.wait_ge(o_scaled, upto(START + n))
                act.activation(o_sb[:, :], acc[:, :], ACT.Copy).then_inc(acc_copied, 1)

            def body(i, last):
                for par in range(2):
                    g = 2 * i + par
                    for s in range(STEPS):
                        exponentials(i, par, s)
                        for j in range(NJ):
                            if s == J_LAST[j] + LAG or s == STEPS - 1 == J_LAST[j]:
                                take_output(i, par, j)
                        for use in MISC.get(s, []):
                            if (s, use) not in uses_of(par, last):
                                continue
                            no, bank = misc_no(i, par, last, s, use), b_bank[bank_no((use, par, s, 0))]
                            if use == "N":
                                shift_rows(g + 2, no, bank)
                            if use[0] == "W":
                                take_rows(g + 2, int(use[1]), no, bank)
                            if use[0] == "T":
                                take_heads(g + 2, int(use[1]), no, bank)
                            if use[0] == "M":
                                j = int(use[1])
                                take_maxima(block_no(g, j), no, bank)
                            if use == "T3":
                                first_part(g + 2)

            with act.Fori(0, GROUPS // 2 - 1) as i:
                body(Turns(i), False)
            body(GROUPS // 2 - 1, True)

        @block.tensor
        def _(pe):
            def by_feature(bank, layer, cols):
                for w, col in enumerate(cols):
                    for k in range(2):
                        for kc in range(2):
                            at = 4 * w + 2 * k
                            ins = pe.matmul(bank[:, at:at + B], wmods[:, layer[w], kc, D * col + P * k:D * col + P * (k + 1)],
                                            cS[:, layer[w], kc, :], start=kc == 0, stop=kc == 1)
                return ins

            pe.wait_ge(dve_step, 3)
            pe.wait_ge(wmod_a_in, 16)
            by_feature(b_bank[0], (0, 0), (0, 1)).then_inc(mod_ready, 1)

            def turn_rows(n, misc=misc):
                pe.wait_ge(xhat_ready, upto(n + 1))
                for k in range(2):
                    for r in range(2):
                        ins = pe.transpose(misc[:, P * (2 * k + r):P * (2 * k + r + 1)], xhat[:, r, P * k:P * (k + 1)], ident[:, :])
                ins.then_inc(misc_filled, 1)

            def project(n, w, misc=misc):
                r, (a, b) = w // 2, ((0, 2 * D), (2 * D, 3 * D))[w % 2]
                if w == 0 and isinstance(n, int) and n == 0:
                    pe.wait_ge(wqkv_in, 16)
                if w == 0:
                    pe.wait_ge(hT_ready, upto(2 * n + 2))
                for k in range(2):
                    ins = pe.matmul(misc[:, 0:b - a], hT[:, k, P * r:P * (r + 1)], wqkv[:, k, a:b], start=k == 0, stop=k == 1)
                ins.then_inc(misc_filled, 1)

            def turn_heads(n, k, misc=misc):
                if k == 0:
                    pe.wait_ge(heads_ready, upto(n + 1))
                for jj in range(4):
                    j = 4 * k + jj
                    ins = pe.transpose(misc[0:80, P * jj:P * (jj + 1)], heads_by_j[:, j, :, :].rearrange("p h d -> p (h d)"), ident[:, :])
                ins.then_inc(misc_filled, 1)

            def turn_maxima(m, misc=misc):
                pe.wait_ge(m_ready, upto(m + 1))
                pe.transpose(misc[:, :].bitcast(BF16)[0:32, 0:P], m_neg[:, :, :, :].rearrange("p h j t -> p (h j t)"), identb[:, :]).then_inc(misc_filled, 1)

            def turn_output(n, misc=misc):
                pe.wait_ge(acc_copied, upto(START + n + 1))
                for t in range(TB):
                    ins = pe.transpose(misc[:, P * t:P * (t + 1)], o_sb[:, P * t:P * (t + 1)], ident[:, :])
                ins.then_inc(misc_filled, 1)

            def emptied(use, n):
                done, count = {"N": (hT_ready, 2 * n + 2), "W": (rows_ready, n + 1), "T": (turned, n + 1),
                               "M": (m_copied, n + 1), "O": (o_scaled, START + n + 1)}[use[0]]
                pe.wait_ge(done, upto(count))

            def number(use, s, g):
                k = int(use[1]) if len(use) > 1 else 0
                return {"N": g + 2, "W": 4 * (g + 2) + k, "T": 4 * (g + 2) + k,
                        "M": block_no(g, k), "O": 4 * g + k}[use[0]]

            def wait_for_bank(i, slot, last):
                was, body_before = occupant(slot, last)
                if body_before and was[0] == "B":
                    pe.wait_ge(b_exped, upto(START + 8 * STEPS * i))
                elif body_before:
                    pe.wait_ge(o_scaled, upto(START + 8 * i))
                elif was[0] == "B":
                    pe.wait_ge(b_exped, upto(START + 8 * STEPS * i + 4 * (STEPS * was[1] + was[2]) + was[3] + 1))
                else:
                    emptied(was[0], number(was[0], was[2], 2 * i + was[1]))

            for n in range(2):
                if n:
                    emptied("W", 4 * n - 1)
                turn_rows(n)
                for w in range(4):
                    emptied("W" if w else "N", 4 * n + w - 1 if w else n)
                    project(n, w)
            for k in range(4):
                emptied("T" if k else "W", k - 1 if k else 7)
                turn_heads(0, k)
            pe.wait_ge(wmod_b_in, 32)
            by_feature(b_bank[1], (0, 0, 1, 1), (3, 4, 0, 1)).then_inc(mod_ready, 1)
            pe.wait_ge(silu_ready, 1)
            for n, (layer, b, cols, _) in enumerate(ROW_MODS):
                if n >= 2:
                    pe.wait_ge(mod_taken, upto(n - 1))
                for w, col in enumerate(cols):
                    for kc in range(2):
                        ins = pe.matmul((b_bank[0], acc)[n % 2][:, D * w:D * (w + 1)], cSb[:, layer, kc, b, :],
                                        wmods[:, layer, kc, D * col:D * (col + 1)], start=kc == 0, stop=kc == 1)
                        if n == w == kc == 0:
                            ins.then_inc(pv_done, START)
                ins.then_inc(mod_ready, 1)
            def score_maxima(i, par, u):
                j, t, c, hp = A_UNITS[u % UNITS]
                buf = (par + u // UNITS) % 2
                w, q = width_a(u % UNITS), C * j + P * t
                unit = UNITS * par + u
                if unit >= LEAD:
                    pe.wait_ge(a_maxed, upto(A_INC * (a_count(i, par, u) - last_use(unit - LEAD, A_RING) + 1)))
                elif unit >= A_RING:
                    pe.wait_ge(a_maxed, upto(A_INC * (unit - A_RING + 1)))
                for k in range(2):
                    ins = pe.matmul(a_bank[unit % A_RING][:, k, 0:w], q_pack[buf][0:KP_ROWS, 2 * hp + k, q:q + P],
                                    k_pack[buf][0:KP_ROWS, C * c:C * c + w], start=True, stop=True)
                ins.then_inc(a_scored, 1)

            def score(i, par, s, h, last):
                j, pieces = B_STEPS[s]
                wait_for_bank(i, ("B", par, s, h), last)
                for kt, at, q in pieces:
                    ins = pe.matmul(b_bank[bank_no(("B", par, s, h))][:, at:at + C - q], k_pack[par][0:KP_ALL, P * kt:P * (kt + 1)],
                                    q_pack[par][0:KP_ALL, h, C * j + q:C * (j + 1)], start=True, stop=True)
                ins.then_inc(b_scored, 1)

            def meet_v(i, par, s):
                j, pieces = B_STEPS[s]
                g = 2 * i + par
                if s == 0:
                    pe.wait_ge(v_in[par], upto(16 * (i + 1)))
                if s == J_FIRST[j]:
                    pe.wait_ge(acc_copied, upto(START + 4 * g + j))
                if s in DIAG:
                    pe.wait_ge(b_masked, upto(2 * (len(DIAG) * g + DIAG.index(s) + 1)))
                else:
                    pe.wait_ge(b_exped, upto(START + 8 * STEPS * i + 4 * (STEPS * par + s) + 4))
                for kt, at, q in pieces:
                    for h in range(QH):
                        ins = pe.matmul(acc[32 * h:32 * (h + 1), q:C], v_tile[par][:, kt, :], probs[:, s % P_RING, h, at:at + C - q],
                                        start=kt == 0, stop=s == J_LAST[j], skip_group_check=True)
                ins.then_inc(pv_done, 1)

            pe.wait_ge(packs_in, upto(16 * PACK_DMAS))
            for u in range(LEAD):
                score_maxima(0, 0, u)
                if u in LEAD_TURN:
                    m = LEAD_TURN[u]
                    emptied("T", 7 if m else 3)
                    turn_maxima(m)
                if u in HEADS_AT:
                    k = HEADS_AT.index(u)
                    emptied("T" if k else "M", 3 + k if k else 0)
                    turn_heads(1, k)

            def body(i, last):
                for par in range(2):
                    g = 2 * i + par
                    for s in range(STEPS):
                        j = B_STEPS[s][0]
                        if s == J_FIRST[j]:
                            pe.wait_ge(m_rows_in, upto(16 * QH * (4 * g + j + 1)))
                        ahead = [u for u in units(s) if not (last and par == 1 and u >= UNITS)]
                        ending = s == STEPS - 1
                        pieces = 2 + (LAG if ending else 0)

                        def maxima(n):
                            for u in share(ahead, n, pieces):
                                if u == UNITS:
                                    pe.wait_ge(packs_in, upto(16 * PACK_DMAS * (g + 2)))
                                score_maxima(i, par, u)

                        score(i, par, s, 0, last)
                        maxima(0)
                        score(i, par, s, 1, last)
                        if s >= LAG:
                            meet_v(i, par, s - LAG)
                        score(i, par, s, 2, last)
                        maxima(1)
                        score(i, par, s, 3, last)
                        if ending:
                            for k in range(LAG):
                                maxima(2 + k)
                                meet_v(i, par, s - LAG + 1 + k)
                        for use in [u for t, u in uses_of(par, last) if t == s]:
                            wait_for_bank(i, (use, par, s, 0), last)
                            n, bank = number(use, s, g), b_bank[bank_no((use, par, s, 0))]
                            if use == "N":
                                turn_rows(n, bank)
                            if use[0] == "W":
                                project(g + 2, int(use[1]), bank)
                            if use[0] == "T":
                                turn_heads(g + 2, int(use[1]), bank)
                            if use[0] == "M":
                                turn_maxima(n, bank)
                            if use[0] == "O":
                                turn_output(n, bank)

            pe.wait_ge(m_copied, len(NEXT))
            with pe.Fori(0, GROUPS // 2 - 1) as i:
                body(Turns(i), False)
            body(GROUPS // 2 - 1, True)


def layer0_out(nc, sems, keep, x, Wproj, fW, fb, fV, fC, w_qkv, w_out, b_out, ln_g, ln_b):
    ident, colmod, rowmod, attn, x2, h1T, w1T, woT, last_rows = keep
    with ExitStack() as ctx:
        def sb(name, shape, dt=F32):
            return ctx.enter_context(nc.sbuf_tensor(name, shape, dt))

        def sem(name):
            return sems.enter_context(nc.semaphore(name))

        wp = sb("wp", [P, 2, D])
        wp_g = sb("wp_g", [P, B, 2, D])
        f_in = sb("f_in", [P, 2, D])
        fv_in = sb("fv_in", [P, 2, 32])
        fc_in = sb("fc_in", [P, 2, 32])
        fvT = sb("fvT", [32, 2, P])
        fcT = sb("fcT", [32, 2, P])
        w_eff = sb("w_eff", [P, B, 2, D])
        wq_in = sb("wq_in", [P, 3, D])
        wo_in = sb("wo_in", [P, 2, P])
        rows_in = sb("rows_in", [P, 4, D])
        f_bias = sb("f_bias", [P, B, D])
        o_in = sb("o_in", [P, B, 2, D])
        aT = sb("aT", [P, B, 2, 2, P])
        y = sb("y", [P, B, 2, D])
        x1 = sb("x1", [P, B, 2, D])
        x1b = sb("x1b", [P, B, 2, D])
        xh = sb("xh", [P, 2, B, 2, D])
        fT = sb("fT", [P, B, 2, 2, P])
        st = sb("st", [P, 2, B, 2, 6])
        mv = sb("mv2", [P, 2, B, 2, 2])
        ve = sb("ve", [P, 2, B, 2])
        rs = sb("rs", [P, 2, B, 2])
        half = sb("half", [P, 2])
        eps = sb("eps", [P, 2])
        bank = [[ctx.enter_context(nc.psum_tensor(f"bank{b}{n}", [P, C], F32)) for n in range(4)] for b in range(B)]

        w_loaded, setup_filled, setup_taken, gated, half_set, x_in = (
            sem("w_loaded"), sem("setup_filled"), sem("setup_taken"), sem("gated"), sem("half_set"), sem("x_in"))
        o_copied, a_turned, a_taken, y_made, y_taken, z_made, x1_made, x1b_made = (
            sem("o_copied"), sem("a_turned"), sem("a_taken"), sem("y_made"), sem("y_taken"), sem("z_made"), sem("x1_made"),
            sem("x1b_made"))
        f_turned, f_taken, f_made, x2_made, h_turned, h_taken = (sem("f_turned"), sem("f_taken"), sem("f_made"), sem("x2_made"),
                                                                sem("h_turned"), sem("h_taken"))
        ln_step = [[sem(f"ln_step{n}{b}") for b in range(B)] for n in range(2)]
        ve_made = [[sem(f"ve_made{n}{b}") for b in range(B)] for n in range(2)]
        rs_made = [[sem(f"rs_made{n}{b}") for b in range(B)] for n in range(2)]
        xh_made = [[sem(f"xh_made{n}{b}") for b in range(B)] for n in range(2)]
        NB = S // ROWS
        GATED = 14

        def run(eng, turn):
            turn(0, True, False, False)
            turn(1, True, True, False)
            turn(2, True, True, True)
            with eng.Fori(3, NB - 1) as n:
                turn(Turns(n), True, True, True)
            turn(NB - 1, True, True, True)
            turn(NB, False, True, True)
            turn(NB + 1, False, False, True)

        def wait_over(eng, s, count):
            if not (isinstance(count, int) and count <= 0):
                eng.wait_ge(s, upto(count))

        block = ctx.enter_context(nc.Block())

        @block.sync
        def _(sp):
            sp.dma_start(wp[:, :, :], Wproj.rearrange("(k p) n -> p k n", p=P)).then_inc(w_loaded, 16)
            sp.dma_start(f_in[:, :, :], fW.rearrange("(k p) n -> p k n", p=P)).then_inc(w_loaded, 16)
            sp.dma_start(fv_in[:, :, :], fV.rearrange("(k p) n -> p k n", p=P)).then_inc(w_loaded, 16)
            sp.dma_start(fc_in[:, :, :], fC.rearrange("(k p) n -> p k n", p=P)).then_inc(w_loaded, 16)
            sp.dma_start(wq_in[:, :, :], w_qkv.rearrange("(k p) n -> p k n", p=P)).then_inc(w_loaded, 16)
            sp.dma_start(wo_in[:, :, :], w_out.rearrange("(k p) n -> p k n", p=P)).then_inc(w_loaded, 16)
            for k, v in enumerate((fb, b_out, ln_g, ln_b)):
                sp.dma_start(rows_in[:, k, :], v.rearrange("(o n) -> o n", o=1).broadcast_to([P, D])).then_inc(w_loaded, 16)
            for b in range(B):
                for k in range(2):
                    sp.dma_start(x2[:, :, b, k, :], x[b, P * NB * k:P * NB * (k + 1), :].rearrange("(c n) d -> c n d", n=NB)) \
                        .then_inc(x_in, 16)

        @block.gpsimd
        def _(pool):
            pool.memset(half[:, :], -0.5).then_inc(half_set, 1)
            pool.memset(eps[:, :], EPS).then_inc(half_set, 1)
            pool.wait_ge(half_set, 2)

            def deviation(n, which, b):
                pool.wait_ge(ln_step[which][b], upto(8 * n + 8))
                pool.tensor_tensor(ve[:, which, b, :], mv[:, which, b, :, 1], eps[:, :], ALU.add).then_inc(ve_made[which][b], 1)
                pool.wait_ge(ve_made[which][b], upto(n + 1))
                pool.tensor_tensor(rs[:, which, b, :], ve[:, which, b, :], half[:, :], ALU.pow).then_inc(rs_made[which][b], 1)

            def turn(n, a, bb, c):
                if a:
                    for b in range(B):
                        deviation(n, 0, b)
                if bb:
                    for b in range(B):
                        deviation(n - 1, 1, b)
                if a:
                    pool.wait_ge(gated, GATED)
                    for b in range(B):
                        pool.wait_ge(x1_made, upto(2 * n + b + 1))
                        wait_over(pool, x2_made, 2 * n + b - 1)
                        pool.tensor_tensor(x1b[:, b, :, :], x1[:, b, :, :], f_bias[:, b, :].unsqueeze(1).broadcast_to([P, 2, D]),
                                           ALU.add).then_inc(x1b_made, 1)

            run(pool, turn)

        @block.vector
        def _(dve):
            def gate(out, in0, in1, op=ALU.mult):
                dve.tensor_tensor(out, in0, in1, op).then_inc(gated, 1)

            dve.wait_ge(w_loaded, 160)
            for b in range(B):
                gate(wp_g[:, b, :, :], wp[:, :, :], rowmod[:, 0, b, :].unsqueeze(1).broadcast_to([P, 2, D]))
                gate(f_bias[:, b, :], rows_in[:, 0, :], rowmod[:, 1, b, :])
                gate(last_rows[:, 0, b, :], rows_in[:, 1, :], rowmod[:, 2, b, :])
                gate(last_rows[:, 1, b, :], rows_in[:, 2, :], rowmod[:, 5, b, :])
                gate(last_rows[:, 2, b, :], rows_in[:, 3, :], rowmod[:, 5, b, :])
            dve.wait_ge(setup_filled, 1)
            dve.tensor_copy(fvT[:, :, :], bank[0][0][0:32, 0:2 * P].rearrange("p (k n) -> p k n", k=2)).then_inc(setup_taken, 1)
            dve.tensor_copy(fcT[:, :, :], bank[0][0][0:32, 2 * P:4 * P].rearrange("p (k n) -> p k n", k=2)).then_inc(setup_taken, 1)
            for k in range(2):
                dve.wait_ge(setup_filled, 2 + k)
                dve.tensor_copy(w1T[:, k, :], bank[0][1 + k][:, 0:3 * P]).then_inc(setup_taken, 1)
            dve.wait_ge(setup_filled, 4)
            for b in range(B):
                dve.tensor_tensor(woT[:, b, :], bank[0][3][:, 0:D], rowmod[:, 2, b, :], ALU.mult).then_inc(setup_taken, 1)
            for k in range(2):
                dve.wait_ge(setup_filled, 5 + k)
                for b in range(B):
                    gate(w_eff[:, b, k, :], bank[1][k][:, 0:D], rowmod[:, 1, b, :])
            dve.wait_ge(x_in, 64)

            def moments(n, which, b, src, made):
                dve.wait_ge(made, upto(2 * n + b + 1))
                for k in range(2):
                    dve.bn_stats(st[:, which, b, k, :], src(k)).then_inc(ln_step[which][b], 2)
                dve.wait_ge(ln_step[which][b], upto(8 * n + 4))
                for k in range(2):
                    dve.bn_aggr(mv[:, which, b, k, :], st[:, which, b, k, :]).then_inc(ln_step[which][b], 2)

            def centre(n, which, b, src, used):
                dve.wait_ge(rs_made[which][b], upto(n + 1))
                wait_over(dve, used, 2 * n + b - 1)
                for k in range(2):
                    ins = dve.tensor_scalar(xh[:, which, b, k, :], src(k), mv[:, which, b, k, 0:1], rs[:, which, b, k:k + 1],
                                            ALU.subtract, ALU.mult)
                ins.then_inc(xh_made[which][b], 1)

            def turn(n, a, bb, c):
                slot = lambda m, b: x2[:, bass.ds(upto(m), 1), b, :, :].rearrange("p m k d -> p (m k) d")
                if a:
                    for b in range(B):
                        dve.wait_ge(z_made, upto(2 * n + b + 1))
                        wait_over(dve, x1b_made, 2 * n + b - 1)
                        dve.tensor_tensor(x1[:, b, :, :], bank[b][0][:, :].rearrange("p (k d) -> p k d", k=2), slot(n, b), ALU.add) \
                            .then_inc(x1_made, 1)
                        moments(n, 0, b, lambda k: x1[:, b, k, :], x1_made)
                    for b in range(B):
                        centre(n, 0, b, lambda k: x1[:, b, k, :], f_turned)
                if bb:
                    m = n - 1
                    for b in range(B):
                        dve.wait_ge(f_made, upto(2 * m + b + 1))
                        dve.wait_ge(x1b_made, upto(2 * m + b + 1))
                        dve.tensor_tensor(slot(m, b), bank[b][1][:, :].rearrange("p (k d) -> p k d", k=2), x1b[:, b, :, :], ALU.add) \
                            .then_inc(x2_made, 1)
                        moments(m, 1, b, lambda k: x2[:, bass.ds(upto(m), 1), b, k, :].rearrange("p m d -> p (m d)"), x2_made)
                    for b in range(B):
                        centre(m, 1, b, lambda k: x2[:, bass.ds(upto(m), 1), b, k, :].rearrange("p m d -> p (m d)"), h_turned)

            run(dve, turn)

        @block.scalar
        def _(act):
            def stage(n):
                for b in range(B):
                    for t in range(2):
                        ins = act.activation(o_in[:, b, t, :].rearrange("p (g e) -> p g e", g=KV).unsqueeze(2),
                                             attn[:, KV * b:KV * (b + 1), bass.ds(upto(2 * n + t), 1), :], ACT.Copy)
                    ins.then_inc(o_copied, 1)

            stage(0)

            def turn(n, a, bb, c):
                if a:
                    for b in range(B):
                        act.wait_ge(a_turned, upto(2 * n + b + 1))
                        act.activation(aT[:, b, :, :, :].rearrange("p k t q -> p (k t q)"), bank[b][0][:, :], ACT.Copy) \
                            .then_inc(a_taken, 1)
                    if not isinstance(n, int) or n + 1 < NB:
                        stage(n + 1)
                    for b in range(B):
                        act.wait_ge(y_made, upto(2 * n + b + 1))
                        act.activation(y[:, b, :, :].rearrange("p t d -> p (t d)"), bank[b][1][:, :], ACT.Copy).then_inc(y_taken, 1)
                if bb:
                    m = n - 1
                    for b in range(B):
                        act.wait_ge(f_turned, upto(2 * m + b + 1))
                        for k in range(2):
                            ins = act.activation(fT[:, b, k, :, :].rearrange("p c q -> p (c q)"), bank[b][3][:, D * k:D * (k + 1)],
                                                 ACT.Identity, bias=colmod[:, 2, k, b:b + 1], scale=colmod[:, 3, k, b:b + 1])
                        ins.then_inc(f_taken, 1)
                if c:
                    m = n - 2
                    for b in range(B):
                        act.wait_ge(h_turned, upto(2 * m + b + 1))
                        for k in range(2):
                            ins = act.activation(h1T[:, b, k, :].rearrange("p (c n) -> p n c", n=NB)[:, bass.ds(upto(m), 1), :],
                                                 bank[b][2][:, D * k:D * (k + 1)].unsqueeze(1), ACT.Identity,
                                                 bias=colmod[:, 4, k, b:b + 1], scale=colmod[:, 5, k, b:b + 1])
                        ins.then_inc(h_taken, 1)

            run(act, turn)

        @block.tensor
        def _(pe):
            pe.wait_ge(w_loaded, 160)
            for k in range(2):
                pe.transpose(bank[0][0][0:32, P * k:P * (k + 1)], fv_in[:, k, :], ident[:, :])
            for k in range(2):
                ins = pe.transpose(bank[0][0][0:32, P * (2 + k):P * (3 + k)], fc_in[:, k, :], ident[:, :])
            ins.then_inc(setup_filled, 1)
            for k in range(2):
                for e in range(3):
                    ins = pe.transpose(bank[0][1 + k][:, P * e:P * (e + 1)], wq_in[:, e, P * k:P * (k + 1)], ident[:, :])
                ins.then_inc(setup_filled, 1)
            for o in range(2):
                ins = pe.transpose(bank[0][3][:, P * o:P * (o + 1)], wo_in[:, o, :], ident[:, :])
            ins.then_inc(setup_filled, 1)
            pe.wait_ge(setup_taken, 2)
            for k in range(2):
                for o in range(2):
                    cols = bank[1][k][:, P * o:P * (o + 1)]
                    pe.matmul(cols, f_in[:, o, P * k:P * (k + 1)], ident[:, :], start=True, stop=False)
                    ins = pe.matmul(cols, fvT[:, k, :], fcT[:, o, :], start=False, stop=True)
                ins.then_inc(setup_filled, 1)
            pe.wait_ge(gated, GATED)
            pe.wait_ge(setup_taken, 6)

            def turn(n, a, bb, c):
                if a:
                    for b in range(B):
                        pe.wait_ge(o_copied, upto(2 * n + b + 1))
                        wait_over(pe, x1_made, 2 * n + b - 1)
                        for k in range(2):
                            for t in range(2):
                                ins = pe.transpose(bank[b][0][:, P * (2 * k + t):P * (2 * k + t + 1)],
                                                   o_in[:, b, t, P * k:P * (k + 1)], ident[:, :])
                        ins.then_inc(a_turned, 1)
                    for b in range(B):
                        pe.wait_ge(a_taken, upto(2 * n + b + 1))
                        wait_over(pe, x2_made, 2 * n + b - 3)
                        for t in range(2):
                            for k in range(2):
                                ins = pe.matmul(bank[b][1][:, D * t:D * (t + 1)], aT[:, b, k, t, :], wp[:, k, :],
                                                start=k == 0, stop=k == 1)
                        ins.then_inc(y_made, 1)
                if bb:
                    m = n - 1
                    for b in range(B):
                        pe.wait_ge(xh_made[0][b], upto(m + 1))
                        wait_over(pe, f_taken, 2 * m + b - 1)
                        for k in range(2):
                            for cc in range(2):
                                ins = pe.transpose(bank[b][3][:, P * (2 * k + cc):P * (2 * k + cc + 1)],
                                                   xh[:, 0, b, cc, P * k:P * (k + 1)], ident[:, :])
                        ins.then_inc(f_turned, 1)
                if a:
                    for b in range(B):
                        pe.wait_ge(y_taken, upto(2 * n + b + 1))
                        for cc in range(2):
                            for t in range(2):
                                ins = pe.matmul(bank[b][0][:, D * cc:D * (cc + 1)], y[:, b, t, P * cc:P * (cc + 1)],
                                                wp_g[:, b, t, :], start=t == 0, stop=t == 1)
                        ins.then_inc(z_made, 1)
                if c:
                    m = n - 2
                    for b in range(B):
                        pe.wait_ge(xh_made[1][b], upto(m + 1))
                        wait_over(pe, h_taken, 2 * m + b - 1)
                        for k in range(2):
                            for cc in range(2):
                                ins = pe.transpose(bank[b][2][:, P * (2 * k + cc):P * (2 * k + cc + 1)],
                                                   xh[:, 1, b, cc, P * k:P * (k + 1)], ident[:, :])
                        ins.then_inc(h_turned, 1)
                if bb:
                    m = n - 1
                    for b in range(B):
                        pe.wait_ge(f_taken, upto(2 * m + b + 1))
                        wait_over(pe, x2_made, 2 * m + b - 1)
                        for cc in range(2):
                            for k in range(2):
                                ins = pe.matmul(bank[b][1][:, D * cc:D * (cc + 1)], fT[:, b, k, cc, :], w_eff[:, b, k, :],
                                                start=k == 0, stop=k == 1)
                        ins.then_inc(f_made, 1)

            run(pe, turn)


def layer1_attention(nc, sems, keep, aoT, v1):
    ident, h1T, w1T, tri = keep
    with ExitStack() as ctx:
        def sb(name, shape, dt=F32):
            return ctx.enter_context(nc.sbuf_tensor(name, shape, dt))

        def sem(name):
            return sems.enter_context(nc.semaphore(name))

        NT = S // P
        PT_RING = 4
        qkT = sb("qkT", [P, B, 2, S])
        p1 = sb("p1", [P, 2, S])
        pT = sb("pT", [P, PT_RING, C])
        mx = sb("mx", [P, 2])
        nm = sb("nm", [P, 2])
        ls = sb("ls", [P, 2, NJ])
        total = sb("total", [P, 2])
        rl = sb("rl", [P, 2])
        ao = sb("ao_rows", [P, 2, P])
        score_banks = ctx.enter_context(nc.psum_tensor("score_banks", [P, 5 * C], F32))
        turn_bank = [ctx.enter_context(nc.psum_tensor(f"turn_bank{n}", [P, C], F32)) for n in range(2)]
        out_bank = ctx.enter_context(nc.psum_tensor("out_bank", [P, C], F32))
        banks = ([score_banks[:, C * n:C * (n + 1)] for n in range(5)] + [t[:, :] for t in turn_bank]
                 + [out_bank[:, :]])
        filled, taken_a, taken_d = sem("filled"), sem("taken_a"), sem("taken_d")
        scored, masked, maxed, negated, exped = sem("scored"), sem("masked"), sem("maxed"), sem("negated"), sem("exped")
        summed, inverted, turned, taken = sem("summed"), sem("inverted"), sem("turned1"), sem("taken")
        multiplied, ao_scaled, ao_turned, ao_taken = sem("multiplied"), sem("ao_scaled"), sem("ao_turned"), sem("ao_taken")

        FILLS = [(b, w, c) for b in range(B) for w in range(3) for c in range(NJ)]
        TASKS = [(b, t) for big in range(NT - 1, NT // 2 - 1, -1) for b in range(B) for t in (big, NT - 1 - big)]
        N = len(TASKS)
        chunks = [-(-(t + 1) // TB) for _, t in TASKS]
        before = [sum(chunks[:u]) for u in range(N + 1)]
        GROUPS_OF_KEYS = [(u, g) for u in range(N) for g in range(chunks[u])]

        TURNS = []
        for n, (u, g) in enumerate(GROUPS_OF_KEYS):
            TURNS += [("keys", n)] + ([("output", u - 1)] if g == chunks[u] - 1 and u else [])
        TURNS.append(("output", N - 1))

        def bank_of(turn):
            return turn_bank[TURNS.index(turn) % 2]

        def region(u):
            first = 0 if u % 2 == 0 else 5 - chunks[u]
            return score_banks[:, C * first:C * (first + chunks[u])]

        def width(u, g):
            return min(C, P * (TASKS[u][1] + 1) - C * g)

        def into(fill):
            b, w, c = fill
            return qkT[:, b, w, C * c:C * (c + 1)] if w < 2 else v1[:, b, TB * c:TB * (c + 1), :].rearrange("p t d -> p (t d)")

        block = ctx.enter_context(nc.Block())

        @block.tensor
        def _(pe):
            for n, (b, w, c) in enumerate(FILLS):
                if n >= 8:
                    pe.wait_ge((taken_a, taken_d)[n % 2], (n - 8) // 2 + 1)
                if w < 2:
                    for k in range(2):
                        ins = pe.matmul(banks[n % 8], w1T[:, k, P * w:P * (w + 1)], h1T[:, b, k, C * c:C * (c + 1)],
                                        start=k == 0, stop=k == 1)
                else:
                    for t in range(TB):
                        for k in range(2):
                            at = C * c + P * t
                            ins = pe.matmul(banks[n % 8][:, P * t:P * (t + 1)], h1T[:, b, k, at:at + P], w1T[:, k, 2 * P:3 * P],
                                            start=k == 0, stop=k == 1)
                ins.then_inc(filled, 1)
            pe.wait_ge(taken_a, len(FILLS) // 2)
            pe.wait_ge(taken_d, len(FILLS) // 2)

            def score(u):
                b, t = TASKS[u]
                if u >= 2:
                    pe.wait_ge(exped, before[u - 1])
                for g in range(chunks[u]):
                    w = width(u, g)
                    ins = pe.matmul(region(u)[:, C * g:C * g + w], qkT[:, b, 0, P * t:P * (t + 1)],
                                    qkT[:, b, 1, C * g:C * g + w], start=True, stop=True)
                ins.then_inc(scored, 1)

            def wait_for_bank(turn):
                at = TURNS.index(turn) - 2
                if at >= 0:
                    what, k = TURNS[at]
                    pe.wait_ge(taken if what == "keys" else ao_taken, k + 1)

            def turn(n):
                u, g = GROUPS_OF_KEYS[n]
                pe.wait_ge(exped, n + 1)
                wait_for_bank(("keys", n))
                for k in range(width(u, g) // P):
                    at = C * g + P * k
                    ins = pe.transpose(bank_of(("keys", n))[:, P * k:P * (k + 1)], p1[:, u % 2, at:at + P], ident[:, :])
                ins.then_inc(turned, 1)

            def multiply(n):
                u, g = GROUPS_OF_KEYS[n]
                b, t = TASKS[u]
                pe.wait_ge(taken, n + 1)
                if g == 0 and u:
                    pe.wait_ge(ao_scaled, u)
                for k in range(width(u, g) // P):
                    kt = TB * g + k
                    ins = pe.matmul(out_bank[:, 0:P], pT[:, n % PT_RING, P * k:P * (k + 1)], v1[:, b, kt, :],
                                    start=kt == 0, stop=kt == t)
                ins.then_inc(multiplied, 1)

            def turn_ao(u):
                pe.wait_ge(ao_scaled, u + 1)
                wait_for_bank(("output", u))
                pe.transpose(bank_of(("output", u))[:, 0:P], ao[:, u % 2, :], ident[:, :]).then_inc(ao_turned, 1)

            score(0)
            score(1)
            for n, (u, g) in enumerate(GROUPS_OF_KEYS):
                turn(n)
                if n:
                    multiply(n - 1)
                if g == 0 and u + 2 < N:
                    score(u + 2)
                if g == chunks[u] - 1 and u:
                    turn_ao(u - 1)
            multiply(len(GROUPS_OF_KEYS) - 1)
            turn_ao(N - 1)

        @block.vector
        def _(dve):
            for n in range(1, len(FILLS), 2):
                dve.wait_ge(filled, n + 1)
                dve.tensor_copy(into(FILLS[n]), banks[n % 8]).then_inc(taken_d, 1)

            def maximum(u):
                w, scores = P * (TASKS[u][1] + 1), region(u)
                dve.wait_ge(scored, u + 1)
                dve.tensor_tensor(scores[:, w - P:w], scores[:, w - P:w], tri, ALU.add).then_inc(masked, 1)
                dve.wait_ge(masked, u + 1)
                dve.tensor_reduce(mx[:, u % 2:u % 2 + 1], scores[:, 0:w], AX.X, ALU.max).then_inc(maxed, 1)
                dve.wait_ge(maxed, u + 1)
                if u >= 2:
                    dve.wait_ge(exped, before[u - 1])
                dve.tensor_scalar(nm[:, u % 2:u % 2 + 1], mx[:, u % 2:u % 2 + 1], -(INNER ** -0.5), None, ALU.mult).then_inc(negated, 1)

            def invert(u):
                dve.wait_ge(exped, before[u + 1])
                dve.tensor_reduce(total[:, u % 2:u % 2 + 1], ls[:, u % 2, 0:chunks[u]], AX.X, ALU.add).then_inc(summed, 1)
                dve.wait_ge(summed, u + 1)
                dve.reciprocal(rl[:, u % 2:u % 2 + 1], total[:, u % 2:u % 2 + 1]).then_inc(inverted, 1)

            def scale(u):
                dve.wait_ge(multiplied, before[u + 1])
                dve.wait_ge(inverted, u + 1)
                if u >= 2:
                    dve.wait_ge(ao_turned, u - 1)
                dve.tensor_scalar(ao[:, u % 2, :], out_bank[:, 0:P], rl[:, u % 2:u % 2 + 1], None, ALU.mult).then_inc(ao_scaled, 1)

            maximum(0)
            maximum(1)
            for u in range(N):
                invert(u)
                if u:
                    scale(u - 1)
                if u + 2 < N:
                    maximum(u + 2)
            scale(N - 1)

        @block.scalar
        def _(act):
            for n in range(0, len(FILLS), 2):
                act.wait_ge(filled, n + 1)
                act.activation(into(FILLS[n]), banks[n % 8], ACT.Copy).then_inc(taken_a, 1)

            def exponential(u, g):
                w = width(u, g)
                if g == 0:
                    act.wait_ge(negated, u + 1)
                    if u >= 2:
                        act.wait_ge(turned, before[u - 1])
                        act.wait_ge(inverted, u - 1)
                act.activation(p1[:, u % 2, C * g:C * g + w], region(u)[:, C * g:C * g + w], ACT.Exp, bias=nm[:, u % 2:u % 2 + 1],
                               scale=INNER ** -0.5, accum_out=ls[:, u % 2, g:g + 1]).then_inc(exped, 1)

            def take(n):
                u, g = GROUPS_OF_KEYS[n]
                w = width(u, g)
                act.wait_ge(turned, n + 1)
                if n >= PT_RING:
                    act.wait_ge(multiplied, n - PT_RING + 1)
                act.activation(pT[:, n % PT_RING, 0:w], bank_of(("keys", n))[:, 0:w], ACT.Copy).then_inc(taken, 1)

            def take_ao(u):
                b, t = TASKS[u]
                act.wait_ge(ao_turned, u + 1)
                act.activation(aoT[:, b, :, HD * t:HD * (t + 1)].rearrange("p n c -> p c n"),
                               bank_of(("output", u))[:, 0:P].rearrange("p (c n) -> p c n", c=HD), ACT.Copy).then_inc(ao_taken, 1)

            for g in range(chunks[0]):
                exponential(0, g)
            for u in range(N):
                ahead = chunks[u + 1] if u + 1 < N else 0
                for g in range(max(chunks[u], ahead)):
                    if g < chunks[u]:
                        take(before[u] + g)
                    if g < ahead:
                        exponential(u + 1, g)
                if u:
                    take_ao(u - 1)
            take_ao(N - 1)


def layer1_out(nc, sems, keep, aoT, out):
    rowmod, x2, woT, last_rows = keep
    with ExitStack() as ctx:
        def sb(name, shape, dt=F32):
            return ctx.enter_context(nc.sbuf_tensor(name, shape, dt))

        def sem(name):
            return sems.enter_context(nc.semaphore(name))

        NB = S // ROWS
        one = sb("one", [1, P])
        ao = sb("ao", [P, B, D])
        x3 = sb("x3", [P, B, 2, D])
        hn = sb("hn", [P, B, 2, D])
        hs = sb("hs", [P, B, 2, D])
        h2 = sb("h2", [P, B, 2, D])
        yn = sb("yn", [P, B, 2, D])
        yg = sb("yg", [P, B, 2, D])
        st = sb("st3", [P, 2, B, 2, 6])
        mv = sb("mv3", [P, 2, B, 2, 2])
        ve = sb("ve3", [P, 2, B, 2])
        rs = sb("rs3", [P, 2, B, 2])
        half = sb("half3", [P, 2])
        eps = sb("eps3", [P, 2])
        zero = sb("zero", [P, 2])
        minus = sb("minus", [P, 2, B, 2])
        shift = sb("shift", [P, 2, B, 2])
        res = sb("res", [P, B, 2, D])
        bank = [ctx.enter_context(nc.psum_tensor(f"o_bank{b}", [P, C], F32)) for b in range(B)]
        consts, staged, projected, x3_made, x3b_made = (sem("consts3"), sem("staged"), sem("projected"), sem("x3_made"),
                                                        sem("x3b_made"))
        ln_step = [[sem(f"s3_{n}{b}") for b in range(B)] for n in range(2)]
        ve_made = [[sem(f"ve3_{n}{b}") for b in range(B)] for n in range(2)]
        rs_made = [[sem(f"rs3_{n}{b}") for b in range(B)] for n in range(2)]
        hn_made, hs_made, h2_made, yn_made, res_made = (sem("hn_made"), sem("hs_made"), sem("h2_made"), sem("yn_made"),
                                                        sem("res_made"))
        yg_made, stored = [sem(f"yg_made{b}") for b in range(B)], [sem(f"stored{b}") for b in range(B)]
        block = ctx.enter_context(nc.Block())

        def run(eng, turn):
            turn(0, True, False, False)
            turn(1, True, True, False)
            turn(2, True, True, True)
            with eng.Fori(3, NB - 1) as n:
                turn(Turns(n), True, True, True)
            turn(NB - 1, True, True, True)
            turn(NB, False, True, True)
            turn(NB + 1, False, False, True)

        def wait_over(eng, s, count):
            if not (isinstance(count, int) and count <= 0):
                eng.wait_ge(s, upto(count))

        def slot(n, b):
            return x2[:, bass.ds(upto(n), 1), b, :, :].rearrange("p m k d -> p (m k) d")

        def gain(eng, m, b):
            eng.wait_ge(yn_made, upto(2 * m + b + 1))
            wait_over(eng, res_made, 2 * m + b - 1)
            eng.tensor_tensor(yg[:, b, :, :], yn[:, b, :, :], last_rows[:, 1, b, :].unsqueeze(1).broadcast_to([P, 2, D]),
                              ALU.mult).then_inc(yg_made[b], 1)

        @block.sync
        def _(sp):
            def store(n):
                for b in range(B):
                    sp.wait_ge(res_made, upto(2 * n + b + 1))
                    sp.dma_start(out[b].rearrange("(k c n) d -> c k n d", c=P, n=NB)[:, :, bass.ds(upto(n), 1), :]
                                 .rearrange("c k n d -> c (k n) d"), res[:, b, :, :]).then_inc(stored[b], 16)

            with sp.Fori(0, NB) as n:
                store(Turns(n))
            for b in range(B):
                sp.wait_ge(stored[b], 16 * NB)

        @block.scalar
        def _(act):
            def centre(n, which, b, dst, src, done):
                act.wait_ge(rs_made[which][b], upto(n + 1))
                for k in range(2):
                    ins = act.activation(dst[:, b, k, :], src[:, b, k, :], ACT.Identity, bias=shift[:, which, b, k:k + 1],
                                         scale=rs[:, which, b, k:k + 1])
                ins.then_inc(done, 1)

            def stage(n):
                for b in range(B):
                    wait_over(act, projected, 2 * n + b - 1)
                    act.activation(ao[:, b, :].unsqueeze(1), aoT[:, b, bass.ds(upto(n), 1), :], ACT.Copy).then_inc(staged, 1)

            stage(0)

            def turn(n, a, bb, c):
                if a and (not isinstance(n, int) or n + 1 < NB):
                    stage(n + 1)
                if a:
                    for b in range(B):
                        wait_over(act, hs_made, 2 * n + b - 1)
                        centre(n, 0, b, hn, x3, hn_made)
                if bb:
                    for b in range(B):
                        wait_over(act, yg_made[b], n - 1)
                        centre(n - 1, 1, b, yn, h2, yn_made)

            run(act, turn)

        @block.tensor
        def _(pe):
            pe.wait_ge(consts, 4)

            def turn(n, a, bb, c):
                if a:
                    for b in range(B):
                        pe.wait_ge(staged, upto(2 * n + b + 1))
                        wait_over(pe, x3_made, 2 * n + b - 1)
                        for k in range(2):
                            cols = bank[b][:, D * k:D * (k + 1)]
                            pe.matmul(cols, ao[:, b, P * k:P * (k + 1)], woT[:, b, :], start=True, stop=False)
                            ins = pe.matmul(cols, one[0:1, :], last_rows[0:1, 0, b, :], start=False, stop=True)
                        ins.then_inc(projected, 1)

            run(pe, turn)

        @block.gpsimd
        def _(pool):
            pool.memset(half[:, :], -0.5).then_inc(consts, 1)
            pool.memset(one[:, :], 1.0).then_inc(consts, 1)
            pool.memset(eps[:, :], EPS).then_inc(consts, 1)
            pool.memset(zero[:, :], 0.0).then_inc(consts, 1)
            pool.wait_ge(consts, 4)

            def deviation(n, which, b):
                pool.wait_ge(ln_step[which][b], upto(8 * n + 8))
                pool.tensor_tensor(ve[:, which, b, :], mv[:, which, b, :, 1], eps[:, :], ALU.add).then_inc(ve_made[which][b], 1)
                pool.tensor_tensor(minus[:, which, b, :], zero[:, :], mv[:, which, b, :, 0], ALU.subtract).then_inc(ve_made[which][b], 1)
                pool.wait_ge(ve_made[which][b], upto(3 * n + 2))
                pool.tensor_tensor(rs[:, which, b, :], ve[:, which, b, :], half[:, :], ALU.pow).then_inc(ve_made[which][b], 1)
                pool.wait_ge(ve_made[which][b], upto(3 * n + 3))
                pool.tensor_tensor(shift[:, which, b, :], minus[:, which, b, :], rs[:, which, b, :], ALU.mult) \
                    .then_inc(rs_made[which][b], 1)

            def turn(n, a, bb, c):
                if a:
                    for b in range(B):
                        deviation(n, 0, b)
                if bb:
                    for b in range(B):
                        deviation(n - 1, 1, b)
                    gain(pool, n - 1, 0)
                if a:
                    for b in range(B):
                        pool.wait_ge(hn_made, upto(2 * n + b + 1))
                        wait_over(pool, h2_made, 2 * n + b - 1)
                        pool.tensor_tensor(hs[:, b, :, :], hn[:, b, :, :], rowmod[:, 4, b, :].unsqueeze(1).broadcast_to([P, 2, D]),
                                           ALU.mult).then_inc(hs_made, 1)

            run(pool, turn)

        @block.vector
        def _(dve):
            def moments(n, which, src, made):
                for b in range(B):
                    dve.wait_ge(made, upto(2 * n + b + 1))
                    for k in range(2):
                        dve.bn_stats(st[:, which, b, k, :], src[:, b, k, :]).then_inc(ln_step[which][b], 2)
                for b in range(B):
                    dve.wait_ge(ln_step[which][b], upto(8 * n + 4))
                    for k in range(2):
                        dve.bn_aggr(mv[:, which, b, k, :], st[:, which, b, k, :]).then_inc(ln_step[which][b], 2)

            def turn(n, a, bb, c):
                m, o = n - 1, n - 2
                if a:
                    for b in range(B):
                        dve.wait_ge(projected, upto(2 * n + b + 1))
                        wait_over(dve, hn_made, 2 * n + b - 1)
                        wait_over(dve, x3b_made, 2 * n + b - 1)
                        dve.tensor_tensor(x3[:, b, :, :], bank[b][:, :].rearrange("p (k d) -> p k d", k=2), slot(n, b), ALU.add) \
                            .then_inc(x3_made, 1)
                    moments(n, 0, x3, x3_made)
                if c:
                    for b in range(B):
                        if b == 1:
                            gain(dve, o, b)
                        dve.wait_ge(yg_made[b], upto(n - 1))
                        wait_over(dve, stored[b], 16 * o)
                        dve.wait_ge(x3b_made, upto(2 * o + b + 1))
                        dve.tensor_tensor(res[:, b, :, :], slot(o, b), yg[:, b, :, :], ALU.add).then_inc(res_made, 1)
                if a:
                    for b in range(B):
                        dve.tensor_tensor(slot(n, b), x3[:, b, :, :], last_rows[:, 2, b, :].unsqueeze(1).broadcast_to([P, 2, D]),
                                          ALU.add).then_inc(x3b_made, 1)
                if bb:
                    for b in range(B):
                        dve.wait_ge(hs_made, upto(2 * m + b + 1))
                        wait_over(dve, yn_made, 2 * m + b - 1)
                        dve.tensor_tensor(h2[:, b, :, :], hs[:, b, :, :], rowmod[:, 3, b, :].unsqueeze(1).broadcast_to([P, 2, D]),
                                          ALU.add).then_inc(h2_made, 1)
                    moments(m, 1, h2, h2_made)

            run(dve, turn)


def adaln_kernel(nc, x, Wqkv, Wproj, lq1, lk1, lq2, lk2, fW, fb, fV, fC, c0, wmod0, w_qkv, w_out, b_out,
                 ln_g, ln_b, c1, wmod1, out):
    with ExitStack() as sems, ExitStack() as ctx:
        def sb(name, shape):
            return ctx.enter_context(nc.sbuf_tensor(name, shape, F32))

        ident = sb("ident", [P, P])
        mask_a = sb("mask_a", [P, C])
        colmod = sb("colmod", [P, 6, 2, B])
        rowmod = sb("rowmod", [P, 6, B, D])
        attn = sb("attn", [P, GROUPS, S // P, 2 * HD])
        layer0_attention(nc, sems, (ident, mask_a, colmod, rowmod, attn), x, Wqkv, lq1, lk1, lq2, lk2, c0, wmod0, c1, wmod1)

        x2 = sb("x2", [P, KV, B, 2, D])
        h1T = sb("h1T", [P, B, 2, S])
        w1T = sb("w1T", [P, 2, 3 * INNER])
        woT = sb("woT", [P, B, D])
        last_rows = sb("last_rows", [P, 3, B, D])
        layer0_out(nc, sems, (ident, colmod, rowmod, attn, x2, h1T, w1T, woT, last_rows), x, Wproj, fW, fb, fV, fC, w_qkv,
                   w_out, b_out, ln_g, ln_b)

        free = attn[:, :, :, :].rearrange("p g t e -> p (g t e)")
        aoT = free[:, 0:B * S].rearrange("p (b n c) -> p b n c", b=B, n=KV)
        v1 = free[:, B * S:2 * B * S].rearrange("p (b t d) -> p b t d", b=B, t=S // P)
        layer1_attention(nc, sems, (ident, h1T, w1T, mask_a[:, C - P:C]), aoT, v1)
        layer1_out(nc, sems, (rowmod, x2, woT, last_rows), aoT, out)


_INS = ["L0_attn_x", "L0_attn_Wqkv", "L0_attn_Wproj", "L0_attn_lambda_q1", "L0_attn_lambda_k1", "L0_attn_lambda_q2",
        "L0_attn_lambda_k2", "L0_ffn_W", "L0_ffn_b", "L0_ffn_V_r", "L0_ffn_C", "L0_c", "L0_wmod", "L1_attn_w_qkv",
        "L1_attn_w_out", "L1_attn_b_out", "L1_ffn_ln_g", "L1_ffn_ln_b", "L1_c", "L1_wmod"]


def kernel(**inputs):
    import concourse.bacc as bacc
    from concourse.bass_utils import run_bass_kernel_spmd

    nc = bacc.Bacc("TRN2", target_bir_lowering=False, num_devices=1)
    arrays, args = {}, []
    for name in _INS:
        a = np.ascontiguousarray(inputs[name])
        arrays[f"in_{name}"] = a
        args.append(nc.dram_tensor(f"in_{name}", a.shape, mybir.dt.from_np(a.dtype), kind="ExternalInput").ap())
    out = nc.dram_tensor("out_0", (B, S, D), F32, kind="ExternalOutput").ap()
    adaln_kernel(nc, *args, out)
    r = run_bass_kernel_spmd(nc, [arrays], core_ids=[0])
    return r.results[0]["out_0"]
```
